# Optimizing a Trainium2 kernel written in Bass

```python
import numpy as np
import jax
import jax.numpy as jnp

def _softmax(x, axis=-1):
    return jax.nn.softmax(x, axis=axis)

def _gelu(x):
    return jax.nn.gelu(x, approximate=True)

def _silu(x):
    return jax.nn.silu(x)

def _sigmoid(x):
    return jax.nn.sigmoid(x)

def _layernorm(x, axis=-1, eps=1e-05):
    m = jnp.mean(x, axis=axis, keepdims=True)
    v = jnp.var(x, axis=axis, keepdims=True)
    return (x - m) / jnp.sqrt(v + eps)

def _scatter_add(tgt, idx, src, axis=0):
    return tgt.at[idx].add(src)

def _segment_sum(src, seg, n):
    return jax.ops.segment_sum(src, seg, n)
kernel_name = 'mk_adaln_ffn_d2_seqx_r8_7aae25'

def setup_inputs(seed: int=0):
    np.random.seed(seed)
    _w = jnp.asarray

    def _rec_inputs():
        import jax
        import jax.numpy as jnp
        _rk = jax.random.key(seed)
        x = -0.000125 + 0.9999 * jax.random.normal(jax.random.fold_in(_rk, 1), (32, 32, 512), jnp.float32)
        _lenS = 32 - jax.random.randint(jax.random.fold_in(_rk, 7), (32,), 0, max(1, 32 // 4) + 1, jnp.int32)
        _lenS2 = 32 - jax.random.randint(jax.random.fold_in(_rk, 8), (32,), 0, max(1, 32 // 4) + 1, jnp.int32)
        condB_codebook = -0.0625 + 0.715345 * jax.random.normal(jax.random.fold_in(_rk, 11), (32,), jnp.float32)
        itok_B_0_23 = jax.random.randint(jax.random.fold_in(_rk, 12), (32,), 0, 24, jnp.int32)
        return (x, condB_codebook, itok_B_0_23)
    x, condB_codebook, itok_B_0_23 = _rec_inputs()

    def _L0_cond_setup():
        import jax, jax.numpy as jnp
        import numpy as np
        GROUP = 128
        LORA_ALPHA = 32.0
        LORA_RANK = 64
        key = jax.random.key(seed)
        k1, k2, k3, k4 = jax.random.split(key, 4)
        O, I = (512, 512)
        x = jax.random.normal(k1, (4, 256, I), dtype=jnp.float32)
        weight = jax.random.normal(k2, (O, I), dtype=jnp.float32) * 0.02
        wg = weight.reshape(O, I // GROUP, GROUP)
        scale_log = jnp.log(jnp.clip(jnp.max(jnp.abs(wg), axis=2, keepdims=True), 1e-05))
        codebook = jnp.array([-1.0, -0.25, 0.0, 1.0], dtype=jnp.float32)
        lora_A = jax.random.normal(k3, (LORA_RANK, I), dtype=jnp.float32) * 0.02
        lora_B = jax.random.normal(k4, (O, LORA_RANK), dtype=jnp.float32) * 0.02
        return {'x': x, 'weight': weight, 'scale_log': scale_log, 'codebook': codebook, 'lora_A': lora_A, 'lora_B': lora_B}
    _L0_cond_all = _L0_cond_setup()
    _L0_cond_in = {k: v for k, v in _L0_cond_all.items() if k in ('weight', 'scale_log', 'lora_A', 'lora_B')}
    del _L0_cond_all

    def _L0_ffn_setup():
        import jax, jax.numpy as jnp
        import numpy as np
        OUT, IN = (512, 512)
        GROUP = 32
        NUM_GROUPS = OUT * IN // GROUP

        def _dequantize_4bit(weight_q4, weight_scale):
            low = weight_q4 & 15
            high = weight_q4 >> 4 & 15
            q8 = jnp.stack([low, high], axis=-1).reshape(weight_q4.shape[0], -1)
            x_norm = q8.astype(jnp.float32) / 15.0
            return x_norm * (2.0 * weight_scale) - weight_scale
        key = jax.random.key(seed)
        k1, k2, k3, k4 = jax.random.split(key, 4)
        x = jax.random.normal(k1, (4, 256, IN), dtype=jnp.float32)
        weight_q4 = jax.random.randint(k2, (NUM_GROUPS, GROUP // 2), 0, 32, dtype=jnp.int32)
        weight_scale = jax.random.uniform(k3, (NUM_GROUPS, 1), dtype=jnp.float32)
        bias = jax.random.normal(k4, (OUT,), dtype=jnp.float32)
        return {'x': x, 'weight_q4': weight_q4, 'weight_scale': weight_scale, 'bias': bias}
    _L0_ffn_all = _L0_ffn_setup()
    _L0_ffn_in = {k: v for k, v in _L0_ffn_all.items() if k in ('weight_q4', 'weight_scale', 'bias')}
    del _L0_ffn_all

    def _L1_cond_setup():
        import jax, jax.numpy as jnp
        import numpy as np
        R = 16
        ALPHA = 32
        SCALING = ALPHA / R
        SLOTS = 32
        IN_F = 512
        OUT_F = 512
        B, T = (8, 128)
        key = jax.random.key(seed)
        k1, k2, k3, k4, k5, k6 = jax.random.split(key, 6)
        x = jax.random.normal(k1, (B, T, IN_F), dtype=jnp.float32)
        adapter_mapping = jax.random.randint(k2, (B,), 0, SLOTS, dtype=jnp.int32)
        W = jax.random.normal(k3, (OUT_F, IN_F), dtype=jnp.float32) * 0.02
        b = jax.random.normal(k4, (OUT_F,), dtype=jnp.float32) * 0.02
        lora_As = jax.random.normal(k5, (SLOTS, IN_F, R), dtype=jnp.float32) * 0.02
        lora_Bs = jax.random.normal(k6, (SLOTS, R, OUT_F), dtype=jnp.float32) * 0.02
        return {'x': x, 'adapter_mapping': adapter_mapping, 'W': W, 'b': b, 'lora_As': lora_As, 'lora_Bs': lora_Bs}
    _L1_cond_all = _L1_cond_setup()
    _L1_cond_in = {k: v for k, v in _L1_cond_all.items() if k in ('W', 'b', 'lora_As', 'lora_Bs')}
    del _L1_cond_all

    def _L1_ffn_setup():
        import jax, jax.numpy as jnp
        import numpy as np
        HD, M = (512, 1792)
        key = jax.random.key(seed)
        k_x, k_g, k_u, k_d = jax.random.split(key, 4)
        scale = 1.0 / np.sqrt(HD)
        x = jax.random.normal(k_x, (4, 256, HD), dtype=jnp.float16)
        W_gate = jax.random.normal(k_g, (M, HD), dtype=jnp.float16) * jnp.float16(scale)
        W_up = jax.random.normal(k_u, (M, HD), dtype=jnp.float16) * jnp.float16(scale)
        W_down = jax.random.normal(k_d, (HD, M), dtype=jnp.float16) * jnp.float16(1.0 / np.sqrt(M))
        return {'x': x, 'W_gate': W_gate, 'W_up': W_up, 'W_down': W_down}
    _L1_ffn_all = _L1_ffn_setup()
    _L1_ffn_in = {k: v for k, v in _L1_ffn_all.items() if k in ('W_gate', 'W_up', 'W_down')}
    del _L1_ffn_all
    return {'x': x, 'condB_codebook': condB_codebook, 'itok_B_0_23': itok_B_0_23, 'L0_cond_weight': _L0_cond_in['weight'], 'L0_cond_scale_log': _L0_cond_in['scale_log'], 'L0_cond_lora_A': _L0_cond_in['lora_A'], 'L0_cond_lora_B': _L0_cond_in['lora_B'], 'L0_ffn_weight_q4': _L0_ffn_in['weight_q4'], 'L0_ffn_weight_scale': _L0_ffn_in['weight_scale'], 'L0_ffn_bias': _L0_ffn_in['bias'], 'L1_cond_W': _L1_cond_in['W'], 'L1_cond_b': _L1_cond_in['b'], 'L1_cond_lora_As': _L1_cond_in['lora_As'], 'L1_cond_lora_Bs': _L1_cond_in['lora_Bs'], 'L1_ffn_W_gate': _L1_ffn_in['W_gate'], 'L1_ffn_W_up': _L1_ffn_in['W_up'], 'L1_ffn_W_down': _L1_ffn_in['W_down']}

def reference(x, condB_codebook, itok_B_0_23, L0_cond_weight, L0_cond_scale_log, L0_cond_lora_A, L0_cond_lora_B, L0_ffn_weight_q4, L0_ffn_weight_scale, L0_ffn_bias, L1_cond_W, L1_cond_b, L1_cond_lora_As, L1_cond_lora_Bs, L1_ffn_W_gate, L1_ffn_W_up, L1_ffn_W_down):
    import jax
    import jax.numpy as jnp

    def _L0_cond_ref(x, weight, scale_log, codebook, lora_A, lora_B):
        import jax, jax.numpy as jnp
        import numpy as np
        GROUP = 128
        LORA_ALPHA = 32.0
        LORA_RANK = 64
        O, I = weight.shape
        lora_delta = lora_B @ lora_A * (LORA_ALPHA / LORA_RANK)
        cb = codebook / jnp.clip(jnp.max(jnp.abs(codebook)), 1e-08)
        scale = jnp.exp(scale_log)
        wg = (weight + lora_delta).reshape(O, I // GROUP, GROUP)
        normalized = wg / scale
        thresholds = (cb[:-1] + cb[1:]) * 0.5
        idx = jnp.searchsorted(thresholds, normalized, side='left')
        quantized = cb[idx]
        w = jax.lax.stop_gradient(quantized - normalized) + normalized
        w_q = (w * scale).reshape(O, I)
        w_eff = w_q + lora_delta
        return x @ w_eff.T

    def _L0_ffn_ref(x, weight_q4, weight_scale, bias):
        import jax, jax.numpy as jnp
        import numpy as np
        OUT, IN = (512, 512)
        GROUP = 32
        NUM_GROUPS = OUT * IN // GROUP

        def _dequantize_4bit(weight_q4, weight_scale):
            low = weight_q4 & 15
            high = weight_q4 >> 4 & 15
            q8 = jnp.stack([low, high], axis=-1).reshape(weight_q4.shape[0], -1)
            x_norm = q8.astype(jnp.float32) / 15.0
            return x_norm * (2.0 * weight_scale) - weight_scale
        w = _dequantize_4bit(weight_q4, weight_scale).reshape(OUT, IN)
        return jnp.einsum('bsi,oi->bso', x, w) + bias

    def _L1_cond_ref(x, adapter_mapping, W, b, lora_As, lora_Bs):
        import jax, jax.numpy as jnp
        import numpy as np
        R = 16
        ALPHA = 32
        SCALING = ALPHA / R
        SLOTS = 32
        IN_F = 512
        OUT_F = 512
        B, T = (8, 128)
        base_out = jnp.einsum('bti,oi->bto', x, W) + b
        A = lora_As[adapter_mapping]
        Bm = lora_Bs[adapter_mapping]
        lora_h = jnp.einsum('bti,bir->btr', x, A)
        lora_out = jnp.einsum('btr,bro->bto', lora_h, Bm)
        return base_out + lora_out * SCALING

    def _L1_ffn_ref(x, W_gate, W_up, W_down):
        import jax, jax.numpy as jnp
        import numpy as np
        HD, M = (512, 1792)
        gate = jnp.einsum('bsh,mh->bsm', x, W_gate)
        up = jnp.einsum('bsh,mh->bsm', x, W_up)
        h = jax.nn.silu(gate) * up
        out = jnp.einsum('bsm,hm->bsh', h, W_down)
        return out
    x = x + _L0_ffn_ref(_L0_cond_ref(x, L0_cond_weight, L0_cond_scale_log, condB_codebook, L0_cond_lora_A, L0_cond_lora_B), L0_ffn_weight_q4, L0_ffn_weight_scale, L0_ffn_bias)
    x = x + _L1_ffn_ref(_L1_cond_ref(x, itok_B_0_23, L1_cond_W, L1_cond_b, L1_cond_lora_As, L1_cond_lora_Bs), L1_ffn_W_gate, L1_ffn_W_up, L1_ffn_W_down)
    return x

_drawn_inputs = setup_inputs


def setup_inputs(seed=0):
    import zlib

    import numpy as np

    out = dict(_drawn_inputs(seed))
    spreads = {}
    factors = {'L1_cond_b': 25.851}
    for name, (base, spread) in spreads.items():
        noise = np.random.default_rng([zlib.crc32(name.encode()), seed]).standard_normal(out[name].shape)
        drawn = base * np.exp(spread * noise) if base else spread * noise
        out[name] = jnp.asarray(drawn.astype(out[name].dtype))
    for name, factor in factors.items():
        out[name] = (out[name] * factor).astype(out[name].dtype)
    return out
```

```python
from contextlib import ExitStack

import concourse.bass as bass
from concourse import mybir

F32 = mybir.dt.float32
F32R = mybir.dt.float32r
F16 = mybir.dt.float16
I32 = mybir.dt.int32
ALU = mybir.AluOpType
ACT = mybir.ActivationFunctionType
AX_X = mybir.AxisListType.X

P = 128
T = 1024
D = 512
KT = D // P
NH = 2
N = T // NH
CODES = 32
CG = 4
RANK0 = 64
LORA0 = 32.0 / 64.0
GRP = 32
R1 = 16
LORA1 = 32.0 / 16.0
SLOTS = 32
B = 32
TB = T // B
GB = P // R1
NG = B // GB
TG = GB * TB
M = 1792
MT = M // P

C_ID = 0
C_BM = C_ID + P
C_TRI = C_BM + TG
C_IOTA = C_TRI + CODES
C_RMOD = C_IOTA + CODES
C_N = C_RMOD + 1


def build_program(nc, a, out):
    ctx = ExitStack()
    with ctx:
        def sb(name, shape, dt, stack=ctx):
            return stack.enter_context(nc.sbuf_tensor(name, shape, dt))

        def sem(name):
            return ctx.enter_context(nc.semaphore(name))

        con = sb("con", [P, C_N], F32)
        ones = sb("ones", [CODES, P], F32)
        codes_in = sb("codes_in", [P, CODES], F32)
        half = sb("half", [P, CODES], F32)
        code = sb("code", [P, CODES], F32)
        absc = sb("absc", [P, CODES], F32)
        peak = sb("peak", [P, 1], F32)
        rpeak = sb("rpeak", [P, 1], F32)
        step = sb("step", [P, CODES], F32)
        bound = sb("bound", [P, CODES + 1], F32)
        fresh = sb("fresh", [P, CODES], F32)
        fbound = sb("fbound", [P, CODES], F32)
        pick = sb("pick", [CODES, 3, CODES], F32)
        rank = sb("rank", [CODES, 1], F32)
        step_c = sb("step_c", [CODES, 1], F32)
        bound_c = sb("bound_c", [CODES, 1], F32)
        place = sb("place", [CODES, 2 * CODES], F32)
        jump = sb("jump", [P, 2 * CODES], F32)
        njump = sb("njump", [P, 1], I32)
        slog = sb("slog", [P, KT * CG], F32)
        scale = sb("scale", [P, KT * CG], F32)
        rscale = sb("rscale", [P, KT * CG], F32)
        bias0 = sb("bias0", [P, KT], F32)
        bias1 = sb("bias1", [P, KT], F32)
        slot = sb("slot", [P, NG], I32)
        row_f = sb("row_f", [P, NG], F32)
        row = sb("row", [P, NG], I32)
        x = sb("x", [P, KT, T], F32)
        wg_raw = sb("wg_raw", [P, KT, M], F16)
        wu_raw = sb("wu_raw", [P, KT, M], F16)
        w1_hi = sb("w1_hi", [P, KT, D], F32R)
        w1_lo = sb("w1_lo", [P, KT, D], F32R)
        ad_hi = sb("ad_hi", [P, KT, D], F32R)
        ad_lo = sb("ad_lo", [P, KT, D], F32R)
        bd_hi = sb("bd_hi", [P, NG, D], F32R)
        bd_lo = sb("bd_lo", [P, NG, D], F32R)

        def zone(name, size, *uses):
            got = []
            for use in uses:
                with ExitStack() as part:
                    got.append([sb(n, s, d, part) for n, s, d in use])
            sb(name, [P, size], F32)
            return got

        (w0, q, w2t, w01), (wc_hi, wc_lo, wd_raw), (gu_w, d_w) = zone(
            "zone_l0", 4 * KT * D,
            [("w0", [P, KT, D], F32), ("q", [P, KT, D], F32), ("w2t", [P, KT, D], F32), ("w01", [P, KT, D], F32)],
            [("wc_hi", [P, KT, D], F32R), ("wc_lo", [P, KT, D], F32R), ("wd_raw", [P, MT, D], F16)],
            [("gu_w", [P, 2, 2, KT, P], F32R), ("d_w", [P, 2, D], F32R)])
        (_, q4, s2, lev, lora_a, lora_b), (x_hi, x_lo), (c_hi, c_lo) = zone(
            "zone_x", 2 * KT * T,
            [("beside_x_hi", [P, KT, T], F32), ("q4", [P, 2, D], I32), ("s2", [P, 2, D], F32),
             ("lev", [P, 2, D], I32), ("lora_a", [RANK0, D], F32), ("lora_b", [RANK0, D], F32)],
            [("x_hi", [P, KT, T], F32R), ("x_lo", [P, KT, T], F32R)],
            [("c_hi", [P, KT, T], F32R), ("c_lo", [P, KT, T], F32R)])
        ((w1_raw, ad_raw, bd_raw, ad_t), (x1_hi, x1_lo), (h, h_hi, h_lo, gact)) = zone(
            "zone_x1", 2 * KT * T,
            [("w1_raw", [P, KT, D], F32), ("ad_raw", [P, NG, D], F32), ("bd_raw", [P, NG, D], F32),
             ("ad_t", [P, KT, D], F32)],
            [("x1_hi", [P, KT, T], F32R), ("x1_lo", [P, KT, T], F32R)],
            [("h", [P, 2, N], F32), ("h_hi", [P, 2, N], F32R), ("h_lo", [P, 2, N], F32R),
             ("gact", [P, 2, N], F32)])
        hit = sb("hit", [P, D], F32)
        ad_m = sb("ad_m", [P, 2 * TG], F32)
        ad_mhi = sb("ad_mhi", [P, 2 * TG], F32R)
        ad_mlo = sb("ad_mlo", [P, 2 * TG], F32R)

        bank = [ctx.enter_context(nc.psum_tensor(f"bank{i}", [P, N], F32)) for i in range(8)]
        delta, wc = bank[0:4], bank[4:8]

        codes_in_ready, con_in, slog_in, lora_in, q4_in, s2_in = (sem(n) for n in (
            "codes_in_ready", "con_in", "slog_in", "lora_in", "q4_in", "s2_in"))
        w0_in = [sem(f"w0_in{i}") for i in range(KT)]
        x_in = [sem(f"x_in{i}") for i in range(KT)]
        w1_in, slot_in, bias_in, gate_up_in, down_in = (sem(n) for n in (
            "w1_in", "slot_in", "bias_in", "gate_up_in", "down_in"))
        ad_in = [sem(f"ad_in{i}") for i in range(NG)]
        bd_in = [sem(f"bd_in{i}") for i in range(NG)]
        stored = sem("stored")
        names = ("tiny", "ones_set", "scale_made", "lora_scaled", "delta_made", "place_made", "jump_made",
                 "levels", "levels_used", "pool_step", "w2t_made", "quant", "w01_made", "row_made", "adt_psum",
                 "adt_made", "x_hi_made", "x_lo_made", "w1_hi_made", "w1_lo_made", "bd_hi_made", "bd_lo_made",
                 "ad_hi_made", "ad_lo_made", "wc_done", "wc_hi_made", "wc_lo_made", "x1_done", "x1_made",
                 "x1_hi_made", "x1_lo_made", "low_done", "ad_m_made", "ad_mhi_made", "ad_mlo_made", "c_done",
                 "c_hi_made", "c_lo_made", "gu_w_made", "d_w_made", "gate_done", "up_done", "gact_made",
                 "h_made", "h_hi_made", "h_lo_made", "down_done", "out_made", "jump_read", "summed")
        s = {n: sem(n) for n in names}

        block = ctx.enter_context(nc.Block())

        @block.sync
        def _(sp):
            sp.dma_start(codes_in[:, :], a["codebook"].to_broadcast([P, CODES])).then_inc(codes_in_ready, 16)
            sp.dma_start(slog[:, :], a["slog"]).then_inc(slog_in, 16)
            sp.dma_start(lora_b[:, :], a["lora_b"]).then_inc(lora_in, 16)
            sp.dma_start(lora_a[:, :], a["lora_a"]).then_inc(lora_in, 16)
            sp.dma_start(con[:, :], a["con"]).then_inc(con_in, 16)
            for t in range(KT):
                sp.dma_start(w0[:, t, :], a["w0"][t]).then_inc(w0_in[t], 16)
                if t == 0:
                    sp.dma_start(slot[:, :], a["slot"]).then_inc(slot_in, 16)
                    sp.dma_start(q4[:, :, :], a["q4"].rearrange("(w p) n -> p w n", p=P)).then_inc(q4_in, 16)
                    for w in range(2):
                        src = a["s2"][w * 8:(w + 1) * 8, :].unsqueeze(1).to_broadcast([8, 16, D])
                        sp.dma_start(s2[:, w, :], src).then_inc(s2_in, 16)
            for k in range(KT):
                sp.dma_start(x[:, k, :], a["x"][k * P:(k + 1) * P, :]).then_inc(x_in[k], 16)
            sp.dma_start(w1_raw[:, :, :], a["w1"].rearrange("(k p) n -> p k n", p=P)).then_inc(w1_in, 16)
            sp.dma_start(bias0[:, :], a["bias0"]).then_inc(bias_in, 16)
            sp.dma_start(bias1[:, :], a["bias1"]).then_inc(bias_in, 16)
            sp.dma_start(wg_raw[:, :, :], a["wg"].rearrange("(k p) m -> p k m", p=P)).then_inc(gate_up_in, 16)
            sp.dma_start(wu_raw[:, :, :], a["wu"].rearrange("(k p) m -> p k m", p=P)).then_inc(gate_up_in, 16)
            sp.wait_ge(s["wc_done"], KT)
            sp.dma_start(wd_raw[:, :, :], a["wd"].rearrange("(t p) n -> p t n", p=P)).then_inc(down_in, 16)
            for i in range(NH * KT):
                n, m = i // KT, i % KT
                sp.wait_ge(s["out_made"], i + 1)
                sp.dma_start(out[m * P:(m + 1) * P, n * N:(n + 1) * N], x[:, m, n * N:(n + 1) * N]).then_inc(stored, 16)
            sp.wait_ge(stored, 16 * NH * KT)

        @block.gpsimd
        def _(pool):
            pool.wait_ge(lora_in, 32)
            pool.tensor_scalar(lora_b[:, :], lora_b[:, :], LORA0, None, ALU.mult).then_inc(s["lora_scaled"], 1)
            for g in range(NG):
                pool.wait_ge(s["row_made"], 1)
                pool.indirect_dma_start(ad_raw[:, g, :], None, a["lora1_a"],
                                        bass.IndirectOffsetOnAxis(ap=row[:, g:g + 1], axis=0)).then_inc(ad_in[g], 16)
            done = 0
            pool.wait_ge(s2_in, 32)
            pool.tensor_scalar(s2[:, :, :], s2[:, :, :], 1.0 / 15.0, None, ALU.mult).then_inc(s["pool_step"], 1)
            done += 1
            for t in range(KT):
                pool.wait_ge(s["levels"], t + 1)
                pool.tensor_scalar(w2t[:, t, :], lev[:, t % 2, :], 2.0, -15.0, ALU.mult, ALU.add
                                   ).then_inc(s["levels_used"], 1)
                pool.wait_ge(s["levels_used"], t + 1)
                pool.wait_ge(s["pool_step"], 1)
                pool.tensor_tensor(w2t[:, t, :], w2t[:, t, :], s2[:, t // 2, :], ALU.mult).then_inc(s["w2t_made"], 1)
            for g in range(NG):
                pool.indirect_dma_start(bd_raw[:, g, :], None, a["lora1_b"],
                                        bass.IndirectOffsetOnAxis(ap=row[:, g:g + 1], axis=0)).then_inc(bd_in[g], 16)
            pool.wait_ge(s["w2t_made"], KT)
            pool.wait_ge(s["delta_made"], KT)
            for k in range(KT):
                pool.wait_ge(s["x_hi_made"], k + 1)
                pool.tensor_tensor(x_lo[:, k, :], x[:, k, :], x_hi[:, k, :].bitcast(F32), ALU.subtract
                                   ).then_inc(s["x_lo_made"], 1)
            for k in range(KT):
                pool.wait_ge(s["ad_hi_made"], k + 1)
                pool.tensor_tensor(ad_lo[:, k, :], ad_t[:, k, :], ad_hi[:, k, :].bitcast(F32), ALU.subtract
                                   ).then_inc(s["ad_lo_made"], 1)
            for k in range(KT):
                pool.wait_ge(s["w1_hi_made"], k + 1)
                pool.tensor_tensor(w1_lo[:, k, :], w1_raw[:, k, :], w1_hi[:, k, :].bitcast(F32), ALU.subtract
                                   ).then_inc(s["w1_lo_made"], 1)
            for g in range(NG):
                pool.wait_ge(s["bd_hi_made"], g + 1)
                pool.tensor_tensor(bd_lo[:, g, :], bd_raw[:, g, :], bd_hi[:, g, :].bitcast(F32), ALU.subtract
                                   ).then_inc(s["bd_lo_made"], 1)

        @block.scalar
        def _(act):
            act.wait_ge(slog_in, 16)
            act.activation(scale[:, :], slog[:, :], ACT.Exp).then_inc(s["scale_made"], 1)
            for k in range(KT):
                act.wait_ge(x_in[k], 16)
                act.activation(x_hi[:, k, :], x[:, k, :], ACT.Copy).then_inc(s["x_hi_made"], 1)
            for k in range(KT):
                act.wait_ge(s["adt_psum"], k + 1)
                act.activation(ad_t[:, k, :], wc[k][:, :], ACT.Copy).then_inc(s["adt_made"], 1)
                act.wait_ge(s["adt_made"], k + 1)
                act.activation(ad_hi[:, k, :], ad_t[:, k, :], ACT.Copy).then_inc(s["ad_hi_made"], 1)
            act.wait_ge(w1_in, 16)
            for k in range(KT):
                act.activation(w1_hi[:, k, :], w1_raw[:, k, :], ACT.Copy).then_inc(s["w1_hi_made"], 1)
            for g in range(NG):
                act.wait_ge(bd_in[g], 16)
                act.activation(bd_hi[:, g, :], bd_raw[:, g, :], ACT.Copy).then_inc(s["bd_hi_made"], 1)
            for k in range(KT):
                act.wait_ge(s["wc_done"], k + 1)
                if k == 0:
                    act.wait_ge(s["quant"], KT)
                act.activation(wc_hi[:, k, :], wc[k][:, :], ACT.Copy).then_inc(s["wc_hi_made"], 1)
            act.wait_ge(s["w1_lo_made"], KT)
            act.wait_ge(s["ad_lo_made"], KT)
            act.wait_ge(s["bd_lo_made"], NG)

            def x1_high(i):
                n, m = i // KT, i % KT
                act.wait_ge(s["x1_made"], i + 1)
                act.activation(x1_hi[:, m, n * N:(n + 1) * N], x[:, m, n * N:(n + 1) * N], ACT.Copy
                               ).then_inc(s["x1_hi_made"], 1)

            def low_high(n):
                act.wait_ge(s["ad_m_made"], n + 1)
                if n:
                    act.wait_ge(s["c_done"], KT)
                act.activation(ad_mhi[:, :], ad_m[:, :], ACT.Copy).then_inc(s["ad_mhi_made"], 1)

            def c_high(i):
                n, m = i // KT, i % KT
                act.wait_ge(s["c_done"], i + 1)
                act.activation(c_hi[:, m, n * N:(n + 1) * N], bank[KT * n + m][:, :], ACT.Identity,
                               bias=bias1[:, m:m + 1]).then_inc(s["c_hi_made"], 1)

            for i in range(NH * KT):
                x1_high(i)
            low_high(0)
            act.wait_ge(bias_in, 32)
            for m in range(KT):
                c_high(m)
            low_high(1)
            act.wait_ge(gate_up_in, 32)

            def gate_weights(u, col, first=False):
                if not first:
                    act.wait_ge(s["gate_done"], u - 1)
                act.activation(gu_w[:, slot_of(u), 0, :, :], wg_raw[:, :, bass.ds(col, P)], ACT.Copy
                               ).then_inc(s["gu_w_made"], 1)

            def up_weights(u, col, first=False):
                if not first:
                    act.wait_ge(s["up_done"], u - 1)
                act.activation(gu_w[:, slot_of(u), 1, :, :], wu_raw[:, :, bass.ds(col, P)], ACT.Copy
                               ).then_inc(s["gu_w_made"], 1)

            def slot_of(u):
                return par[0]

            par = [0]
            for u in range(2):
                par[0] = u
                gate_weights(u, u * P, True)
                up_weights(u, u * P, True)
            for m in range(KT, 2 * KT):
                c_high(m)

            def hidden(u, col2, parity, more=True):
                par[0] = parity
                act.wait_ge(s["gate_done"], u + 1)
                if not (isinstance(u, int) and u < 2):
                    act.wait_ge(s["h_made"], u - 1)
                act.activation(gact[:, parity, :], bank[2 * parity][:, :], ACT.Silu).then_inc(s["gact_made"], 1)
                if more:
                    gate_weights(u + 2, col2)
                act.wait_ge(s["h_made"], u + 1)
                if not (isinstance(u, int) and u < 2):
                    act.wait_ge(s["down_done"], u - 1)
                act.activation(h_hi[:, parity, :], h[:, parity, :], ACT.Copy).then_inc(s["h_hi_made"], 1)
                if more:
                    up_weights(u + 2, col2)

            act.wait_ge(s["c_done"], 2 * KT)
            for n in range(NH):
                base = n * MT
                hidden(base, 2 * P, 0)
                hidden(base + 1, 3 * P, 1)
                with act.Fori(1, MT // 2 - 1) as i:
                    hidden(base + 2 * i, i * (2 * P) + 2 * P, 0)
                    hidden(base + 2 * i + 1, i * (2 * P) + 3 * P, 1)
                hidden(base + MT - 2, 0, 0, n == 0)
                hidden(base + MT - 1, P, 1, n == 0)

        @block.vector
        def _(dve):
            steps = [0]

            def link(ins):
                steps[0] += 1
                ins.then_inc(s["tiny"], 1)
                dve.wait_ge(s["tiny"], steps[0])

            dve.memset(ones[:, :], 1.0).then_inc(s["ones_set"], 1)
            dve.memset(bound[:, 0:1], -2.0)
            dve.memset(bound[:, CODES:CODES + 1], 2.0)
            dve.memset(step[:, CODES - 1:CODES], 0.0)
            link(dve.memset(fresh[:, CODES - 1:CODES], 0.0))
            dve.wait_ge(codes_in_ready, 16)
            link(dve.scalar_tensor_tensor(out=absc[:, :], in0=codes_in[:, :], scalar=-1.0, in1=codes_in[:, :],
                                          op0=ALU.mult, op1=ALU.max))
            link(dve.tensor_reduce(peak[:, :], absc[:, :], AX_X, ALU.max))
            link(dve.tensor_scalar(peak[:, :], peak[:, :], 1e-8, None, ALU.max))
            link(dve.reciprocal(rpeak[:, :], peak[:, :]))
            dve.tensor_scalar(code[:, :], codes_in[:, :], rpeak[:, 0:1], None, ALU.mult)
            link(dve.tensor_scalar(half[:, :], codes_in[:, :], rpeak[:, 0:1], 0.5, ALU.mult, ALU.mult))
            dve.tensor_tensor(step[:, 0:CODES - 1], code[:, 1:CODES], code[:, 0:CODES - 1], ALU.subtract)
            link(dve.tensor_tensor(bound[:, 1:CODES], half[:, 0:CODES - 1], half[:, 1:CODES], ALU.add))
            d = CODES // 4
            while d:
                mid = bound[:, d:CODES:2 * d]
                link(dve.tensor_tensor(mid, mid, bound[:, 0:CODES - d:2 * d], ALU.max))
                link(dve.tensor_tensor(mid, mid, bound[:, 2 * d:CODES + 1:2 * d], ALU.min))
                d //= 2
            link(dve.tensor_tensor(fresh[:, 0:CODES - 1], bound[:, 1:CODES], bound[:, 0:CODES - 1], ALU.is_gt))
            link(dve.tensor_reduce(peak[:, :], fresh[:, :], AX_X, ALU.add))
            dve.tensor_scalar(njump[:, :], peak[:, :], -1.0, 1.0, ALU.add, ALU.max)
            link(dve.tensor_tensor(fbound[:, :], bound[:, 1:CODES + 1], fresh[:, :], ALU.mult))
            dve.wait_ge(con_in, 16)
            for i, (col, src, mask) in enumerate(((rank, fresh, C_TRI), (step_c, step, C_ID), (bound_c, fbound, C_ID))):
                ins = dve.scalar_tensor_tensor(out=pick[:, i, :], in0=src[0:CODES, :], scalar=1.0,
                                               in1=con[0:CODES, mask:mask + CODES], op0=ALU.mult, op1=ALU.mult,
                                               accum_out=col[:, :])
            link(ins)
            iota = con[0:CODES, C_IOTA:C_IOTA + CODES]
            dve.tensor_scalar(place[:, 0:CODES], iota, rank[:, 0:1], bound_c[:, 0:1], ALU.is_equal, ALU.mult)
            dve.tensor_scalar(place[:, CODES:2 * CODES], iota, rank[:, 0:1], step_c[:, 0:1], ALU.is_equal,
                              ALU.mult).then_inc(s["place_made"], 1)
            dve.wait_ge(slot_in, 16)
            link(dve.tensor_scalar(row_f[:, :], slot[:, :], float(R1), con[:, C_RMOD:C_RMOD + 1], ALU.mult, ALU.add))
            dve.tensor_copy(row[:, :], row_f[:, :]).then_inc(s["row_made"], 1)
            dve.wait_ge(s["scale_made"], 1)
            link(dve.reciprocal(rscale[:, :], scale[:, :]))
            dve.wait_ge(s["jump_made"], 1)
            dve.tensor_copy(jump[:, :], bank[7][:, 0:2 * CODES]).then_inc(s["jump_read"], 1)
            dve.wait_ge(s["jump_read"], 1)
            dve.wait_ge(q4_in, 16)

            def levels(t):
                if t >= 2:
                    dve.wait_ge(s["levels_used"], t - 1)
                w, high = t // 2, t % 2
                if high:
                    dve.tensor_scalar(lev[:, t % 2, :], q4[:, w, :], 4, 15, ALU.logical_shift_right,
                                      ALU.bitwise_and).then_inc(s["levels"], 1)
                else:
                    dve.tensor_scalar(lev[:, t % 2, :], q4[:, w, :], 15, None, ALU.bitwise_and
                                      ).then_inc(s["levels"], 1)

            levels(0)
            levels(1)
            more = dve.value_load(njump[0:1, 0:1], min_val=1, max_val=CODES - 2)

            for t in range(KT):
                dve.wait_ge(w0_in[t], 16)
                dve.wait_ge(s["delta_made"], t + 1)
                link(dve.tensor_tensor(q[:, t, :], w0[:, t, :], delta[t][:, :], ALU.add))
                rs = rscale[:, t * CG:(t + 1) * CG].unsqueeze(2).to_broadcast([P, CG, P])
                sc = scale[:, t * CG:(t + 1) * CG].unsqueeze(2).to_broadcast([P, CG, P])
                q3 = q[:, t, :].rearrange("p (g n) -> p g n", g=CG)
                w3 = w01[:, t, :].rearrange("p (g n) -> p g n", g=CG)
                link(dve.tensor_tensor(q3, q3, rs, ALU.mult))
                link(dve.tensor_scalar(w01[:, t, :], q[:, t, :], jump[:, 0:1], jump[:, CODES:CODES + 1],
                                       ALU.is_gt, ALU.mult))
                with dve.Fori(0, more) as j:
                    before = more * (2 * t) + 2 * j
                    dve.tensor_scalar(hit[:, :], q[:, t, :], jump[:, bass.ds(j + 1, 1)],
                                      jump[:, bass.ds(j + CODES + 1, 1)],
                                      ALU.is_gt, ALU.mult).then_inc(s["summed"], 1)
                    dve.wait_ge(s["summed"], before + 1)
                    dve.tensor_tensor(w01[:, t, :], w01[:, t, :], hit[:, :], ALU.add).then_inc(s["summed"], 1)
                    dve.wait_ge(s["summed"], before + 2)
                link(dve.scalar_tensor_tensor(out=w3, in0=w3, scalar=code[:, 0:1], in1=sc, op0=ALU.add, op1=ALU.mult))
                dve.tensor_tensor(w01[:, t, :], w01[:, t, :], delta[t][:, :], ALU.add).then_inc(s["quant"], 1)
                if t + 2 < KT:
                    levels(t + 2)

            for k in range(KT):
                dve.wait_ge(s["wc_hi_made"], k + 1)
                if k == 0:
                    dve.wait_ge(s["quant"], KT)
                dve.tensor_tensor(wc_lo[:, k, :], wc[k][:, :], wc_hi[:, k, :].bitcast(F32), ALU.subtract
                                  ).then_inc(s["wc_lo_made"], 1)

            def x1_sum(i):
                n, m = i // KT, i % KT
                at = x[:, m, n * N:(n + 1) * N]
                dve.wait_ge(s["x1_done"], i + 1)
                dve.scalar_tensor_tensor(out=at, in0=bank[KT * n + m][:, :], scalar=bias0[:, m:m + 1], in1=at,
                                         op0=ALU.add, op1=ALU.add).then_inc(s["x1_made"], 1)

            def x1_low(i):
                n, m = i // KT, i % KT
                dve.wait_ge(s["x1_hi_made"], i + 1)
                dve.tensor_tensor(x1_lo[:, m, n * N:(n + 1) * N], x[:, m, n * N:(n + 1) * N],
                                  x1_hi[:, m, n * N:(n + 1) * N].bitcast(F32), ALU.subtract).then_inc(s["x1_lo_made"], 1)

            def low_mask(n):
                dve.wait_ge(s["low_done"], n + 1)
                if n:
                    dve.wait_ge(s["ad_mlo_made"], 1)
                mask = con[:, C_BM:C_BM + TG].unsqueeze(1).to_broadcast([P, 2, TG])
                dve.tensor_tensor(ad_m[:, :].rearrange("p (g t) -> p g t", g=2),
                                  bank[KT * n + 3][:, :].rearrange("p (g t) -> p g t", g=2), mask, ALU.mult
                                  ).then_inc(s["ad_m_made"], 1)
                dve.wait_ge(s["ad_mhi_made"], n + 1)
                dve.tensor_tensor(ad_mlo[:, :], ad_m[:, :], ad_mhi[:, :].bitcast(F32), ALU.subtract
                                  ).then_inc(s["ad_mlo_made"], 1)

            def c_low(i):
                n, m = i // KT, i % KT
                dve.wait_ge(s["c_hi_made"], i + 1)
                dve.scalar_tensor_tensor(out=c_lo[:, m, n * N:(n + 1) * N], in0=bank[KT * n + m][:, :],
                                         scalar=bias1[:, m:m + 1], in1=c_hi[:, m, n * N:(n + 1) * N].bitcast(F32),
                                         op0=ALU.add, op1=ALU.subtract).then_inc(s["c_lo_made"], 1)

            dve.wait_ge(bias_in, 32)
            for n in range(NH):
                for i in range(n * KT, (n + 1) * KT):
                    x1_sum(i)
                    if i % KT:
                        x1_low(i - 1)
                x1_low((n + 1) * KT - 1)
            low_mask(0)
            for m in range(KT):
                c_low(m)
            low_mask(1)

            def down_weights(u, parity, t):
                if not (isinstance(u, int) and u < 2):
                    dve.wait_ge(s["down_done"], u - 1)
                dve.tensor_copy(d_w[:, parity, :].unsqueeze(1), wd_raw[:, bass.ds(t, 1), :]).then_inc(s["d_w_made"], 1)

            for m in range(KT, 2 * KT):
                c_low(m)
            dve.wait_ge(down_in, 16)
            dve.wait_ge(s["c_done"], 2 * KT)

            def hidden(u, t, parity):
                dve.wait_ge(s["gact_made"], u + 1)
                dve.wait_ge(s["up_done"], u + 1)
                if not (isinstance(u, int) and u < 2):
                    dve.wait_ge(s["h_lo_made"], u - 1)
                dve.tensor_tensor(h[:, parity, :], gact[:, parity, :], bank[2 * parity + 1][:, :], ALU.mult
                                  ).then_inc(s["h_made"], 1)
                down_weights(u, parity, t)
                dve.wait_ge(s["h_hi_made"], u + 1)
                dve.tensor_tensor(h_lo[:, parity, :], h[:, parity, :], h_hi[:, parity, :].bitcast(F32), ALU.subtract
                                  ).then_inc(s["h_lo_made"], 1)

            def out_sum(n):
                for m in range(KT):
                    at = x[:, m, n * N:(n + 1) * N]
                    dve.wait_ge(s["down_done"], (n + 1) * MT)
                    dve.tensor_tensor(at, bank[KT + m][:, :], at, ALU.add).then_inc(s["out_made"], 1)

            for n in range(NH):
                base = n * MT
                hidden(base, 0, 0)
                if n:
                    out_sum(n - 1)
                hidden(base + 1, 1, 1)
                with dve.Fori(1, MT // 2) as i:
                    hidden(base + 2 * i, 2 * i, 0)
                    hidden(base + 2 * i + 1, 2 * i + 1, 1)
            out_sum(NH - 1)

        @block.tensor
        def _(pe):
            pe.wait_ge(s["ones_set"], 1)
            pe.wait_ge(s["place_made"], 1)
            pe.matmul(bank[7][:, 0:2 * CODES], ones[:, :], place[:, :], start=True, stop=True).then_inc(s["jump_made"], 1)
            pe.wait_ge(s["lora_scaled"], 1)
            for t in range(KT):
                pe.matmul(delta[t][:, :], lora_b[:, t * P:(t + 1) * P], lora_a[:, :], start=True, stop=True
                          ).then_inc(s["delta_made"], 1)
            pe.wait_ge(con_in, 16)
            pe.wait_ge(s["jump_read"], 1)
            for g in range(NG):
                pe.wait_ge(ad_in[g], 16)
            for k in range(KT):
                for g in range(NG):
                    mm = pe.transpose(wc[k][:, g * P:(g + 1) * P], ad_raw[:, g, k * P:(k + 1) * P],
                                      con[:, C_ID:C_ID + P])
                mm.then_inc(s["adt_psum"], 1)
            for t in range(KT):
                pe.wait_ge(s["quant"], t + 1)
                pe.wait_ge(s["w2t_made"], t + 1)
                for k in range(KT):
                    if t == 0:
                        pe.wait_ge(s["adt_made"], k + 1)
                    mm = pe.matmul(wc[k][:, :], w01[:, t, k * P:(k + 1) * P], w2t[:, t, :], start=(t == 0),
                                   stop=(t == KT - 1))
                    if t == KT - 1:
                        mm.then_inc(s["wc_done"], 1)

            def three(dst, w_hi, w_lo, v_hi, v_lo, start, stop):
                pe.matmul(dst, w_hi, v_hi, start=start, stop=False)
                pe.matmul(dst, w_hi, v_lo, start=False, stop=False)
                return pe.matmul(dst, w_lo, v_hi, start=False, stop=stop)

            pe.wait_ge(s["x_lo_made"], KT)
            for k in range(KT):
                pe.wait_ge(s["wc_hi_made"], k + 1)
                pe.wait_ge(s["wc_lo_made"], k + 1)
                for m in range(KT):
                    mm = three(bank[m][:, :], wc_hi[:, k, m * P:(m + 1) * P], wc_lo[:, k, m * P:(m + 1) * P],
                               x_hi[:, k, 0:N], x_lo[:, k, 0:N], k == 0, k == KT - 1)
                    if k == KT - 1:
                        mm.then_inc(s["x1_done"], 1)
            for m in range(KT):
                for k in range(KT):
                    mm = three(bank[KT + m][:, :], wc_hi[:, k, m * P:(m + 1) * P], wc_lo[:, k, m * P:(m + 1) * P],
                               x_hi[:, k, N:T], x_lo[:, k, N:T], k == 0, k == KT - 1)
                mm.then_inc(s["x1_done"], 1)

            for n in range(NH):
                pe.wait_ge(s["x1_lo_made"], (n + 1) * KT)
                for gg in range(2):
                    g = 2 * n + gg
                    for k in range(KT):
                        mm = three(bank[KT * n + 3][:, gg * TG:(gg + 1) * TG], ad_hi[:, k, g * P:(g + 1) * P],
                                   ad_lo[:, k, g * P:(g + 1) * P], x1_hi[:, k, g * TG:(g + 1) * TG],
                                   x1_lo[:, k, g * TG:(g + 1) * TG], k == 0, k == KT - 1)
                mm.then_inc(s["low_done"], 1)
                for m in range(KT):
                    if m == KT - 1:
                        pe.wait_ge(s["ad_m_made"], n + 1)
                    for k in range(KT):
                        three(bank[KT * n + m][:, :], w1_hi[:, k, m * P:(m + 1) * P], w1_lo[:, k, m * P:(m + 1) * P],
                              x1_hi[:, k, n * N:(n + 1) * N], x1_lo[:, k, n * N:(n + 1) * N], k == 0, False)
                    pe.wait_ge(s["ad_mlo_made"], n + 1)
                    for gg in range(2):
                        g = 2 * n + gg
                        mm = three(bank[KT * n + m][:, gg * TG:(gg + 1) * TG], bd_hi[:, g, m * P:(m + 1) * P],
                                   bd_lo[:, g, m * P:(m + 1) * P], ad_mhi[:, gg * TG:(gg + 1) * TG],
                                   ad_mlo[:, gg * TG:(gg + 1) * TG], False, gg == 1)
                    mm.then_inc(s["c_done"], 1)

            def gate_up(u, parity, n):
                tok = slice(n * N, (n + 1) * N)
                for part in range(2):
                    pe.wait_ge(s["gu_w_made"], 2 * u + part + 1)
                    if not (isinstance(u, int) and u < 2):
                        if part == 0:
                            pe.wait_ge(s["h_made"], u - 1)
                    for k in range(KT):
                        w = gu_w[:, parity, part, k, :]
                        pe.matmul(bank[2 * parity + part][:, :], w, c_hi[:, k, tok], start=(k == 0), stop=False)
                        mm = pe.matmul(bank[2 * parity + part][:, :], w, c_lo[:, k, tok], start=False,
                                       stop=(k == KT - 1))
                    mm.then_inc(s["up_done" if part else "gate_done"], 1)

            def down(u, parity, first=False, last=False):
                pe.wait_ge(s["d_w_made"], u + 1)
                pe.wait_ge(s["h_hi_made"], u + 1)
                pe.wait_ge(s["h_lo_made"], u + 1)
                for m in range(KT):
                    w = d_w[:, parity, m * P:(m + 1) * P]
                    pe.matmul(bank[KT + m][:, :], w, h_hi[:, parity, :], start=first, stop=False,
                              skip_group_check=True)
                    mm = pe.matmul(bank[KT + m][:, :], w, h_lo[:, parity, :], start=False, stop=last,
                                   skip_group_check=True)
                mm.then_inc(s["down_done"], 1)

            for n in range(NH):
                base = n * MT
                if n == 0:
                    pe.wait_ge(s["c_lo_made"], 2 * KT)
                    gate_up(0, 0, 0)
                gate_up(base + 1, 1, n)
                if n:
                    pe.wait_ge(s["out_made"], KT)
                down(base, 0, first=True)
                with pe.Fori(1, MT // 2) as i:
                    gate_up(base + 2 * i, 0, n)
                    down(base + 2 * i - 1, 1)
                    gate_up(base + 2 * i + 1, 1, n)
                    down(base + 2 * i, 0)
                if n + 1 < NH:
                    gate_up(base + MT, 0, n + 1)
                down(base + MT - 1, 1, last=True)


def host_constants(np):
    con = np.zeros((P, C_N), np.float32)
    con[:, C_ID:C_ID + P] = np.eye(P)
    rows, toks = np.arange(P)[:, None], np.arange(TG)[None, :]
    con[:, C_BM:C_BM + TG] = np.where(rows // R1 == toks // TB, LORA1, 0.0)
    con[:CODES, C_TRI:C_TRI + CODES] = np.tril(np.ones((CODES, CODES)))
    con[:, C_IOTA:C_IOTA + CODES] = np.arange(1, CODES + 1)
    con[:, C_RMOD] = np.arange(P) % R1
    return con


def kernel(**inputs):
    import numpy as np
    import concourse.bacc as bacc
    from concourse import mybir as mb
    from concourse.bass_utils import run_bass_kernel_spmd as run

    v = {k: np.asarray(x) for k, x in inputs.items()}
    arrays = {
        "codebook": v["condB_codebook"].reshape(1, CODES),
        "slog": v["L0_cond_scale_log"].reshape(2, P, 2, CG).transpose(1, 0, 2, 3).reshape(P, KT * CG),
        "lora_a": v["L0_cond_lora_A"],
        "lora_b": v["L0_cond_lora_B"].reshape(2, P, 2, RANK0).transpose(3, 0, 2, 1).reshape(RANK0, D),
        "con": host_constants(np),
        "w0": v["L0_cond_weight"].reshape(2, P, 2, D).transpose(0, 2, 1, 3).reshape(KT, P, D),
        "slot": np.repeat(v["itok_B_0_23"], R1).reshape(NG, P).T,
        "q4": v["L0_ffn_weight_q4"].reshape(D, D // 2).T,
        "s2": v["L0_ffn_weight_scale"].reshape(D, D // GRP).T,
        "x": v["x"].reshape(T, D).T,
        "w1": v["L1_cond_W"].T,
        "bias0": v["L0_ffn_bias"].reshape(KT, P).T,
        "bias1": v["L1_cond_b"].reshape(KT, P).T,
        "lora1_a": v["L1_cond_lora_As"].transpose(0, 2, 1).reshape(SLOTS * R1, D),
        "lora1_b": v["L1_cond_lora_Bs"].reshape(SLOTS * R1, D),
        "wg": v["L1_ffn_W_gate"].T,
        "wu": v["L1_ffn_W_up"].T,
        "wd": v["L1_ffn_W_down"].T,
    }
    arrays = {k: np.ascontiguousarray(x) for k, x in arrays.items()}
    nc = bacc.Bacc("TRN2", target_bir_lowering=False, num_devices=1)
    aps = {k: nc.dram_tensor("in_" + k, x.shape, mb.dt.from_np(x.dtype), kind="ExternalInput").ap()
           for k, x in arrays.items()}
    out = nc.dram_tensor("out_t", (D, T), mb.dt.float32, kind="ExternalOutput").ap()
    build_program(nc, aps, out)
    got = run(nc, [{"in_" + k: x for k, x in arrays.items()}], core_ids=[0]).results[0]["out_t"]
    return np.ascontiguousarray(np.asarray(got).T).reshape(B, TB, D)
```

```python
from contextlib import ExitStack

import concourse.bass as bass
from concourse import mybir

F32 = mybir.dt.float32
F32R = mybir.dt.float32r
F16 = mybir.dt.float16
BF16 = mybir.dt.bfloat16
I32 = mybir.dt.int32
ALU = mybir.AluOpType
ACT = mybir.ActivationFunctionType
AX_X = mybir.AxisListType.X

P = 128
T = 1024
D = 512
KT = D // P
NH = 2
N = T // NH
CODES = 32
CG = 4
RANK0 = 64
LORA0 = 32.0 / 64.0
GRP = 32
WARM_START = 10
R1 = 16
LORA1 = 32.0 / 16.0
SLOTS = 32
B = 32
TB = T // B
GB = P // R1
NG = B // GB
TG = GB * TB
M = 1792
MT = M // P

C_ID = 0
C_BM = C_ID + P
C_TRI = C_BM + TG
C_IOTA = C_TRI + CODES
C_N = C_IOTA + CODES

DELTA_ORDER = (3, 0, 1, 2)
FIRST = ((0, 0), (0, 3), (1, 0), (1, 3), (0, 1), (0, 2), (1, 1), (1, 2))
FIRST_OF_0 = 6


def build_program(nc, a, out):
    ctx = ExitStack()
    with ctx:
        def sb(name, shape, dt, stack=ctx):
            return stack.enter_context(nc.sbuf_tensor(name, shape, dt))

        def sem(name):
            return ctx.enter_context(nc.semaphore(name))

        con = sb("con", [P, C_N], F32)
        ones = sb("ones", [CODES, P], F32)
        codes_in = sb("codes_in", [P, CODES], F32)
        half = sb("half", [P, CODES], F32)
        code = sb("code", [P, CODES], F32)
        absc = sb("absc", [P, CODES], F32)
        peak = sb("peak", [P, 1], F32)
        rpeak = sb("rpeak", [P, 1], F32)
        step = sb("step", [P, CODES], F32)
        bound = sb("bound", [P, CODES + 1], F32)
        fresh = sb("fresh", [P, CODES], F32)
        fbound = sb("fbound", [P, CODES], F32)
        pick = sb("pick", [CODES, 3, CODES], F32)
        rank = sb("rank", [CODES, 1], F32)
        step_c = sb("step_c", [CODES, 1], F32)
        bound_c = sb("bound_c", [CODES, 1], F32)
        place = sb("place", [CODES, 2 * CODES], F32)
        jump = sb("jump", [P, 2 * CODES], F32)
        jump_hi = sb("jump_hi", [P, CODES], F32R)
        jump_lo = sb("jump_lo", [P, CODES], F32)
        njump = sb("njump", [P, 1], I32)
        npairs = sb("npairs", [P, 1], I32)
        diag = sb("diag", [P, 2, 2, P], F32R)
        slog = sb("slog", [P, KT * CG], F32)
        scale = sb("scale", [P, KT * CG], F32)
        rscale = sb("rscale", [P, KT * CG], F32)
        bias0 = sb("bias0", [P, KT], F32)
        bias1 = sb("bias1", [P, KT], F32)
        slot = sb("slot", [P, NG + 1], I32)
        spare = sb("spare", [CODES, 2], F32)
        row16 = sb("row16", [P, NG], I32)
        row = sb("row", [P, NG], I32)
        x = sb("x", [P, KT, T], F32)
        wg_raw = sb("wg_raw", [P, KT, M], F16)
        wu_raw = sb("wu_raw", [P, KT, M], F16)
        w1_hi = sb("w1_hi", [P, KT, D], F32R)
        w1_lo = sb("w1_lo", [P, KT, D], F32R)
        bd_hi = sb("bd_hi", [P, NG, D], F32R)
        bd_lo = sb("bd_lo", [P, NG, D], F32R)

        def zone(name, size, *uses):
            got = []
            for use in uses:
                with ExitStack() as part:
                    got.append([sb(n, s, d, part) for n, s, d in use])
            sb(name, [P, size], F32)
            return got

        (w2t_hi, w2t_lo), (ad_m, ad_mhi, ad_mlo) = zone(
            "zone_w2t", 2 * (KT - 1) * D,
            [("w2t_hi", [P, KT - 1, D], F32R), ("w2t_lo", [P, KT - 1, D], F32R)],
            [("ad_m", [P, 2 * TG], F32), ("ad_mhi", [P, 2 * TG], F32R), ("ad_mlo", [P, 2 * TG], F32R)])
        (above,), (w01_hi, w01_lo), (ad_hi, ad_lo) = zone(
            "zone_above", 2 * KT * D,
            [("above", [P, 2, KT, D], F32R)],
            [("w01_hi", [P, KT - 1, D], F32R), ("w01_lo", [P, KT - 1, D], F32R)],
            [("ad_hi", [P, KT, D], F32R), ("ad_lo", [P, KT, D], F32R)])
        (w0, q, w2t, dsb), (w01,), (wc_hi, wc_lo, wd_raw), (gu_w, d_w) = zone(
            "zone_l0", 4 * KT * D,
            [("w0", [P, KT, D], F32), ("q", [P, KT, D], F32), ("w2t", [P, KT, D], F32), ("dsb", [P, KT, D], F32)],
            [("w01", [P, KT, D], F32)],
            [("wc_hi", [P, KT, D], F32R), ("wc_lo", [P, KT, D], F32R), ("wd_raw", [P, MT, D], F16)],
            [("gu_w", [P, 2, 2, KT, P], F32R), ("d_w", [P, 2, D], F32R)])
        (lora_a, lora_b, idle, _, q4, s2, lev), (x_hi, x_lo), (c_hi, c_lo) = zone(
            "zone_x", 2 * KT * T,
            [("lora_a", [RANK0, D], F32), ("lora_b", [RANK0, D], F32), ("idle", [P, N], BF16),
             ("beside_x_hi", [P, KT * T - 2 * D - N // 2], F32),
             ("q4", [P, 2, D], I32), ("s2", [P, 2, D], F32), ("lev", [P, KT, D], I32)],
            [("x_hi", [P, KT, T], F32R), ("x_lo", [P, KT, T], F32R)],
            [("c_hi", [P, KT, T], F32R), ("c_lo", [P, KT, T], F32R)])
        ((w1_raw, ad_raw, bd_raw, ad_t), (x1_hi, x1_lo), (h, h_hi, h_lo, gact)) = zone(
            "zone_x1", 2 * KT * T,
            [("w1_raw", [P, KT, D], F32), ("ad_raw", [P, NG, D], F32), ("bd_raw", [P, NG, D], F32),
             ("ad_t", [P, KT, D], F32)],
            [("x1_hi", [P, KT, T], F32R), ("x1_lo", [P, KT, T], F32R)],
            [("h", [P, 2, N], F32), ("h_hi", [P, 2, N], F32R), ("h_lo", [P, 2, N], F32R),
             ("gact", [P, 2, N], F32)])

        bank = [ctx.enter_context(nc.psum_tensor(f"bank{i}", [P, N], F32)) for i in range(8)]
        acc, delta, wc = bank[0:4], bank[4:8], bank[4:8]

        codes_in_ready, con_in, slog_in, lora_in, q4_in, s2_in = (sem(n) for n in (
            "codes_in_ready", "con_in", "slog_in", "lora_in", "q4_in", "s2_in"))
        w0_in = [sem(f"w0_in{i}") for i in range(KT)]
        x_in = [sem(f"x_in{i}") for i in range(KT)]
        w1_in, slot_in, bias_in, gate_up_in, down_in = (sem(n) for n in (
            "w1_in", "slot_in", "bias_in", "gate_up_in", "down_in"))
        ad_in = [sem(f"ad_in{i}") for i in range(NG)]
        bd_in = [sem(f"bd_in{i}") for i in range(NG)]
        stored = sem("stored")
        names = ("tiny", "ones_set", "idle_set", "sum_done", "scale_made", "rscale_made", "delta_made", "dsb_made", "q_sum", "q_made", "above_first", "above_made", "diag_made", "acc_used", "place_made", "jump_made",
                 "levels", "levels_used", "w2t_made", "quant", "quant_first", "w01_hi_made", "w01_lo_made", "w2t_hi_made", "w2t_lo_made", "row_made", "adt_psum",
                 "adt_made", "x_hi_made", "x_lo_made", "w1_hi_made", "w1_lo_made", "bd_hi_made", "bd_lo_made",
                 "ad_hi_made", "ad_lo_made", "wc_done", "wc_hi_made", "wc_lo_made", "x1_done", "x1_made",
                 "x1_hi_made", "x1_lo_made", "low_done", "ad_m_made", "ad_mhi_made", "ad_mlo_made", "c_done",
                 "c_hi_made", "c_lo_made", "gu_w_made", "d_w_made", "gate_done", "up_done", "gact_made",
                 "h_made", "h_hi_made", "h_lo_made", "down_done", "out_made", "jump_read", "split_made", "pairs_made")
        s = {n: sem(n) for n in names}

        block = ctx.enter_context(nc.Block())

        @block.sync
        def _(sp):
            sp.dma_start(codes_in[:, :], a["codebook"].to_broadcast([P, CODES])).then_inc(codes_in_ready, 16)
            sp.dma_start(lora_b[:, :], a["lora_b"]).then_inc(lora_in, 16)
            sp.dma_start(w0[:, 0, :], a["w0"][0]).then_inc(w0_in[0], 16)
            sp.dma_start(con[:, :], a["con"]).then_inc(con_in, 16)
            for t in range(1, KT):
                sp.dma_start(w0[:, t, :], a["w0"][t]).then_inc(w0_in[t], 16)
            for g in range(NG):
                sp.wait_ge(ad_in[g], 16)
            sp.dma_start(q4[:, :, :], a["q4"].rearrange("(w p) n -> p w n", p=P)).then_inc(q4_in, 16)
            for w in range(2):
                src = a["s2"][w * 8:(w + 1) * 8, :].unsqueeze(1).to_broadcast([8, 16, D])
                sp.dma_start(s2[:, w, :], src).then_inc(s2_in, 16)
            for k in range(KT):
                sp.dma_start(x[:, k, :], a["x"][k * P:(k + 1) * P, :]).then_inc(x_in[k], 16)
            sp.dma_start(w1_raw[:, :, :], a["w1"].rearrange("(k p) n -> p k n", p=P)).then_inc(w1_in, 16)
            sp.dma_start(bias0[:, :], a["bias0"]).then_inc(bias_in, 16)
            sp.dma_start(bias1[:, :], a["bias1"]).then_inc(bias_in, 16)
            for g in range(NG):
                sp.wait_ge(bd_in[g], 16)
            sp.dma_start(wg_raw[:, :, :], a["wg"].rearrange("(k p) m -> p k m", p=P)).then_inc(gate_up_in, 16)
            sp.dma_start(wu_raw[:, :, :], a["wu"].rearrange("(k p) m -> p k m", p=P)).then_inc(gate_up_in, 16)
            sp.wait_ge(s["wc_done"], KT)
            sp.dma_start(wd_raw[:, :, :], a["wd"].rearrange("(t p) n -> p t n", p=P)).then_inc(down_in, 16)
            for i in range(NH * KT):
                n, m = i // KT, i % KT
                sp.wait_ge(s["out_made"], i + 1)
                sp.dma_start(out[m * P:(m + 1) * P, n * N:(n + 1) * N], x[:, m, n * N:(n + 1) * N]).then_inc(stored, 16)
            sp.wait_ge(stored, 16 * NH * KT)

        @block.gpsimd
        def _(pool):
            pool.wait_ge(slot_in, 16)
            pool.tensor_scalar(row16[:, :], slot[:, 0:NG], float(R1), 0.0, ALU.mult, ALU.add).then_inc(s["row_made"], 1)
            pool.wait_ge(s["row_made"], 1)
            pool.tensor_tensor(row[:, :], row16[:, :], slot[:, NG:NG + 1].to_broadcast([P, NG]), ALU.add
                               ).then_inc(s["row_made"], 1)
            pool.wait_ge(s["row_made"], 2)
            for g in range(NG):
                pool.indirect_dma_start(ad_raw[:, g, :], None, a["lora1_a"],
                                        bass.IndirectOffsetOnAxis(ap=row[:, g:g + 1], axis=0)).then_inc(ad_in[g], 16)
            for i, t in enumerate((3, 2)):
                pool.wait_ge(w0_in[t], 16)
                pool.wait_ge(s["dsb_made"], DELTA_ORDER.index(t) + 1)
                pool.tensor_tensor(q[:, t, :], w0[:, t, :], dsb[:, t, :], ALU.add).then_inc(s["q_sum"], 1)
                pool.wait_ge(s["q_sum"], i + 1)
                pool.wait_ge(s["rscale_made"], 1)
                q3 = q[:, t, :].rearrange("p (g n) -> p g n", g=CG)
                rs = rscale[:, t * CG:(t + 1) * CG].unsqueeze(2).to_broadcast([P, CG, P])
                pool.tensor_tensor(q3, q3, rs, ALU.mult).then_inc(s["q_made"], 1)
            for g in range(NG):
                pool.indirect_dma_start(bd_raw[:, g, :], None, a["lora1_b"],
                                        bass.IndirectOffsetOnAxis(ap=row[:, g:g + 1], axis=0)).then_inc(bd_in[g], 16)
            pool.wait_ge(s2_in, 32)
            def w2t_low(t):
                pool.wait_ge(s["w2t_hi_made"], t)
                pool.tensor_tensor(w2t_lo[:, t - 1, :], w2t[:, t, :], w2t_hi[:, t - 1, :].bitcast(F32), ALU.subtract
                                   ).then_inc(s["w2t_lo_made"], 1)

            for t in range(KT):
                pool.wait_ge(s["levels"], t + 1)
                pool.tensor_scalar(w2t[:, t, :], lev[:, t, :], 2.0, -15.0, ALU.mult, ALU.add
                                   ).then_inc(s["levels_used"], 1)
                pool.wait_ge(s["levels_used"], t + 1)
                pool.tensor_tensor(w2t[:, t, :], w2t[:, t, :], s2[:, t // 2, :], ALU.mult).then_inc(s["w2t_made"], 1)
                if t > 1:
                    w2t_low(t - 1)
            w2t_low(KT - 1)
            for k in range(KT):
                pool.wait_ge(s["w1_hi_made"], k + 1)
                pool.tensor_tensor(w1_lo[:, k, :], w1_raw[:, k, :], w1_hi[:, k, :].bitcast(F32), ALU.subtract
                                   ).then_inc(s["w1_lo_made"], 1)
            for g in range(NG):
                pool.wait_ge(s["bd_hi_made"], g + 1)
                pool.tensor_tensor(bd_lo[:, g, :], bd_raw[:, g, :], bd_hi[:, g, :].bitcast(F32), ALU.subtract
                                   ).then_inc(s["bd_lo_made"], 1)

        @block.scalar
        def _(act):
            act.dma_start(slot[:, :], a["slot"]).then_inc(slot_in, 16)
            act.dma_start(lora_a[:, :], a["lora_a"]).then_inc(lora_in, 16)
            act.dma_start(slog[:, :], a["slog"]).then_inc(slog_in, 16)
            act.wait_ge(s["ones_set"], 1)
            act.activation(spare[:, 0:1], ones[:, 0:1], ACT.Exp)
            act.wait_ge(slog_in, 16)
            act.activation(scale[:, :], slog[:, :], ACT.Exp).then_inc(s["scale_made"], 1)
            for i, t in enumerate(DELTA_ORDER):
                act.wait_ge(s["delta_made"], i + 1)
                act.activation(dsb[:, t, :], delta[t][:, :], ACT.Copy, scale=LORA0).then_inc(s["dsb_made"], 1)

            def diagonal(e, col, parity):
                if not (isinstance(e, int) and e < 2):
                    act.wait_ge(s["acc_used"], KT * (e - 1))
                for i, part in enumerate((jump, jump_lo)):
                    at = col + CODES if i == 0 else col
                    act.activation(diag[:, parity, i, :], con[:, C_ID:C_ID + P], ACT.Copy,
                                   scale=part[:, bass.ds(at, 1)]).then_inc(s["diag_made"], 1)

            act.wait_ge(con_in, 16)
            act.wait_ge(s["split_made"], 1)
            act.wait_ge(s["pairs_made"], 1)
            diagonal(0, 0, 0)
            diagonal(1, 1, 1)
            pairs = act.value_load(npairs[0:1, 0:1], min_val=1, max_val=CODES // 2 - 1)
            act.wait_ge(s["acc_used"], FIRST_OF_0)
            with act.Fori(0, pairs) as j:
                diagonal(2 * j + 2, 2 * j + 2, 0)
                diagonal(2 * j + 3, 2 * j + 3, 1)
            for k in range(KT):
                act.wait_ge(s["adt_psum"], k + 1)
                act.activation(ad_t[:, k, :], wc[k][:, :], ACT.Copy).then_inc(s["adt_made"], 1)
            act.wait_ge(s["acc_used"], KT * (2 * pairs + 2))
            for t in range(1, KT):
                act.wait_ge(s["w2t_made"], t + 1)
                act.activation(w2t_hi[:, t - 1, :], w2t[:, t, :], ACT.Copy).then_inc(s["w2t_hi_made"], 1)
                act.wait_ge(s["quant"], t + 1)
                act.activation(w01_hi[:, t - 1, :], w01[:, t, :], ACT.Copy).then_inc(s["w01_hi_made"], 1)
            act.wait_ge(s["delta_made"], KT)
            for k in range(KT):
                act.wait_ge(x_in[k], 16)
                act.activation(x_hi[:, k, :], x[:, k, :], ACT.Copy).then_inc(s["x_hi_made"], 1)
            for k in range(KT):
                act.wait_ge(s["wc_done"], k + 1)
                act.wait_ge(s["w01_lo_made"], KT - 1)
                act.activation(wc_hi[:, k, :], wc[k][:, :], ACT.Copy, scale=1.0 / 15.0).then_inc(s["wc_hi_made"], 1)
            act.wait_ge(w1_in, 16)
            for k in range(KT):
                act.activation(w1_hi[:, k, :], w1_raw[:, k, :], ACT.Copy).then_inc(s["w1_hi_made"], 1)
            for g in range(NG):
                act.wait_ge(bd_in[g], 16)
                act.activation(bd_hi[:, g, :], bd_raw[:, g, :], ACT.Copy).then_inc(s["bd_hi_made"], 1)
            for k in range(KT):
                act.wait_ge(s["adt_made"], k + 1)
                act.activation(ad_hi[:, k, :], ad_t[:, k, :], ACT.Copy).then_inc(s["ad_hi_made"], 1)
            act.activation(spare[:, 1:2], ones[:, 0:1], ACT.Silu)
            act.wait_ge(s["w1_lo_made"], KT)
            act.wait_ge(s["ad_lo_made"], KT)
            act.wait_ge(s["bd_lo_made"], NG)

            def x1_high(i):
                n, m = i // KT, i % KT
                act.wait_ge(s["x1_made"], i + 1)
                act.activation(x1_hi[:, m, n * N:(n + 1) * N], x[:, m, n * N:(n + 1) * N], ACT.Copy
                               ).then_inc(s["x1_hi_made"], 1)

            def low_high(n):
                act.wait_ge(s["ad_m_made"], n + 1)
                if n:
                    act.wait_ge(s["c_done"], KT)
                act.activation(ad_mhi[:, :], ad_m[:, :], ACT.Copy).then_inc(s["ad_mhi_made"], 1)

            def c_high(i):
                n, m = i // KT, i % KT
                act.wait_ge(s["c_done"], i + 1)
                act.activation(c_hi[:, m, n * N:(n + 1) * N], bank[KT * n + m][:, :], ACT.Identity,
                               bias=bias1[:, m:m + 1]).then_inc(s["c_hi_made"], 1)

            for i in range(NH * KT):
                x1_high(i)
            low_high(0)
            act.wait_ge(bias_in, 32)
            for m in range(KT):
                c_high(m)
            low_high(1)
            act.wait_ge(gate_up_in, 32)

            def gate_weights(u, col, first=False):
                if not first:
                    act.wait_ge(s["gate_done"], u - 1)
                act.activation(gu_w[:, slot_of(u), 0, :, :], wg_raw[:, :, bass.ds(col, P)], ACT.Copy
                               ).then_inc(s["gu_w_made"], 1)

            def up_weights(u, col, first=False):
                if not first:
                    act.wait_ge(s["up_done"], u - 1)
                act.activation(gu_w[:, slot_of(u), 1, :, :], wu_raw[:, :, bass.ds(col, P)], ACT.Copy
                               ).then_inc(s["gu_w_made"], 1)

            def slot_of(u):
                return par[0]

            par = [0]
            for u in range(2):
                par[0] = u
                gate_weights(u, u * P, True)
                up_weights(u, u * P, True)
            for m in range(KT, 2 * KT):
                c_high(m)

            def hidden(u, col2, parity, more=True):
                par[0] = parity
                act.wait_ge(s["gate_done"], u + 1)
                if not (isinstance(u, int) and u < 2):
                    act.wait_ge(s["h_made"], u - 1)
                act.activation(gact[:, parity, :], bank[2 * parity][:, :], ACT.Silu).then_inc(s["gact_made"], 1)
                if more:
                    gate_weights(u + 2, col2)
                act.wait_ge(s["h_made"], u + 1)
                if not (isinstance(u, int) and u < 2):
                    act.wait_ge(s["down_done"], u - 1)
                act.activation(h_hi[:, parity, :], h[:, parity, :], ACT.Copy).then_inc(s["h_hi_made"], 1)
                if more:
                    up_weights(u + 2, col2)

            act.wait_ge(s["c_done"], 2 * KT)
            for n in range(NH):
                base = n * MT
                hidden(base, 2 * P, 0)
                hidden(base + 1, 3 * P, 1)
                with act.Fori(1, MT // 2 - 1) as i:
                    hidden(base + 2 * i, i * (2 * P) + 2 * P, 0)
                    hidden(base + 2 * i + 1, i * (2 * P) + 3 * P, 1)
                hidden(base + MT - 2, 0, 0, n == 0)
                hidden(base + MT - 1, P, 1, n == 0)

        @block.vector
        def _(dve):
            steps = [0]

            def link(ins):
                steps[0] += 1
                ins.then_inc(s["tiny"], 1)
                dve.wait_ge(s["tiny"], steps[0])

            dve.memset(idle[:, :], 0.0).then_inc(s["idle_set"], 1)
            dve.memset(ones[:, :], 1.0).then_inc(s["ones_set"], 1)
            dve.memset(bound[:, 0:1], -2.0)
            dve.memset(bound[:, CODES:CODES + 1], 2.0)
            dve.memset(step[:, CODES - 1:CODES], 0.0)
            link(dve.memset(fresh[:, CODES - 1:CODES], 0.0))
            dve.wait_ge(codes_in_ready, 16)
            link(dve.scalar_tensor_tensor(out=absc[:, :], in0=codes_in[:, :], scalar=-1.0, in1=codes_in[:, :],
                                          op0=ALU.mult, op1=ALU.max))
            link(dve.tensor_reduce(peak[:, :], absc[:, :], AX_X, ALU.max))
            link(dve.tensor_scalar(peak[:, :], peak[:, :], 1e-8, None, ALU.max))
            link(dve.reciprocal(rpeak[:, :], peak[:, :]))
            dve.tensor_scalar(code[:, :], codes_in[:, :], rpeak[:, 0:1], None, ALU.mult)
            link(dve.tensor_scalar(half[:, :], codes_in[:, :], rpeak[:, 0:1], 0.5, ALU.mult, ALU.mult))
            dve.tensor_tensor(step[:, 0:CODES - 1], code[:, 1:CODES], code[:, 0:CODES - 1], ALU.subtract)
            link(dve.tensor_tensor(bound[:, 1:CODES], half[:, 0:CODES - 1], half[:, 1:CODES], ALU.add))
            d = CODES // 4
            while d:
                mid = bound[:, d:CODES:2 * d]
                link(dve.tensor_tensor(mid, mid, bound[:, 0:CODES - d:2 * d], ALU.max))
                link(dve.tensor_tensor(mid, mid, bound[:, 2 * d:CODES + 1:2 * d], ALU.min))
                d //= 2
            link(dve.tensor_tensor(fresh[:, 0:CODES - 1], bound[:, 1:CODES], bound[:, 0:CODES - 1], ALU.is_gt))
            link(dve.tensor_reduce(peak[:, :], fresh[:, :], AX_X, ALU.add))
            dve.tensor_scalar(njump[:, :], peak[:, :], -1.0, 2.0, ALU.add, ALU.max)
            link(dve.tensor_tensor(fbound[:, :], bound[:, 1:CODES + 1], fresh[:, :], ALU.mult))
            dve.wait_ge(con_in, 16)
            for i, (col, src, mask) in enumerate(((rank, fresh, C_TRI), (step_c, step, C_ID), (bound_c, fbound, C_ID))):
                ins = dve.scalar_tensor_tensor(out=pick[:, i, :], in0=src[0:CODES, :], scalar=1.0,
                                               in1=con[0:CODES, mask:mask + CODES], op0=ALU.mult, op1=ALU.mult,
                                               accum_out=col[:, :])
            link(ins)
            iota = con[0:CODES, C_IOTA:C_IOTA + CODES]
            dve.tensor_scalar(place[:, 0:CODES], iota, rank[:, 0:1], bound_c[:, 0:1], ALU.is_equal, ALU.mult)
            dve.tensor_scalar(place[:, CODES:2 * CODES], iota, rank[:, 0:1], step_c[:, 0:1], ALU.is_equal,
                              ALU.mult).then_inc(s["place_made"], 1)
            dve.tensor_scalar(npairs[:, :], njump[:, :], 1, None, ALU.logical_shift_right).then_inc(s["pairs_made"], 1)
            dve.wait_ge(s["scale_made"], 1)
            dve.reciprocal(rscale[:, :], scale[:, :]).then_inc(s["rscale_made"], 1)
            dve.wait_ge(s["jump_made"], 1)
            dve.tensor_copy(jump[:, :], bank[3][:, 0:2 * CODES]).then_inc(s["jump_read"], 1)
            dve.wait_ge(s["jump_read"], 1)
            link(dve.tensor_copy(jump_hi[:, :], jump[:, CODES:2 * CODES]))
            dve.tensor_tensor(jump_lo[:, :], jump[:, CODES:2 * CODES], jump_hi[:, :].bitcast(F32), ALU.subtract
                              ).then_inc(s["split_made"], 1)

            def normalise(t):
                dve.wait_ge(w0_in[t], 16)
                dve.wait_ge(s["dsb_made"], DELTA_ORDER.index(t) + 1)
                link(dve.tensor_tensor(q[:, t, :], w0[:, t, :], dsb[:, t, :], ALU.add))
                if t == 0:
                    dve.wait_ge(s["rscale_made"], 1)
                rs = rscale[:, t * CG:(t + 1) * CG].unsqueeze(2).to_broadcast([P, CG, P])
                q3 = q[:, t, :].rearrange("p (g n) -> p g n", g=CG)
                link(dve.tensor_tensor(q3, q3, rs, ALU.mult))

            for e, t in FIRST:
                if e == 0:
                    if t < 2:
                        normalise(t)
                    else:
                        dve.wait_ge(s["q_made"], 4 - t)
                dve.tensor_scalar(above[:, e, t, :], q[:, t, :], jump[:, e:e + 1], None, ALU.is_gt
                                  ).then_inc(s["above_first"], 1)

            def compare(e, col, parity):
                dve.wait_ge(s["acc_used"], KT * (e - 1))
                for half_ in range(2):
                    two = slice(2 * half_, 2 * half_ + 2)
                    dve.tensor_scalar(above[:, parity, two, :], q[:, two, :], jump[:, bass.ds(col, 1)], None,
                                      ALU.is_gt).then_inc(s["above_made"], 1)

            def level(t):
                w, high = t // 2, t % 2
                if high:
                    dve.tensor_scalar(lev[:, t, :], q4[:, w, :], 4, 15, ALU.logical_shift_right,
                                      ALU.bitwise_and).then_inc(s["levels"], 1)
                else:
                    dve.tensor_scalar(lev[:, t, :], q4[:, w, :], 15, None, ALU.bitwise_and
                                      ).then_inc(s["levels"], 1)

            pairs = dve.value_load(npairs[0:1, 0:1], min_val=1, max_val=CODES // 2 - 1)
            dve.wait_ge(q4_in, 16)
            level(0)
            level(1)
            dve.wait_ge(s["acc_used"], FIRST_OF_0)
            with dve.Fori(0, pairs) as j:
                compare(2 * j + 2, 2 * j + 2, 0)
                compare(2 * j + 3, 2 * j + 3, 1)
            level(2)
            level(3)
            def w01_low(t):
                dve.wait_ge(s["w01_hi_made"], t)
                dve.tensor_tensor(w01_lo[:, t - 1, :], w01[:, t, :], w01_hi[:, t - 1, :].bitcast(F32), ALU.subtract
                                  ).then_inc(s["w01_lo_made"], 1)

            def weight(t, groups):
                dve.wait_ge(s["acc_used"], KT * (2 * pairs + 1) + t + 1)
                n = groups.stop - groups.start
                at = slice(groups.start * P, groups.stop * P)
                sc = scale[:, t * CG + groups.start:t * CG + groups.stop].unsqueeze(2).to_broadcast([P, n, P])
                link(dve.scalar_tensor_tensor(out=w01[:, t, at].rearrange("p (g n) -> p g n", g=n),
                                              in0=acc[t][:, at].rearrange("p (g n) -> p g n", g=n),
                                              scalar=code[:, 0:1], in1=sc, op0=ALU.add, op1=ALU.mult))
                return dve.tensor_tensor(w01[:, t, at], w01[:, t, at], dsb[:, t, at], ALU.add)

            weight(0, slice(0, CG // 2)).then_inc(s["quant_first"], 1)
            weight(0, slice(CG // 2, CG)).then_inc(s["quant"], 1)
            weight(1, slice(0, CG)).then_inc(s["quant"], 1)
            for t in range(2, KT):
                weight(t, slice(0, CG)).then_inc(s["quant"], 1)
                w01_low(t - 1)
            w01_low(KT - 1)
            dve.wait_ge(s["w2t_made"], KT)
            for k in range(KT):
                dve.wait_ge(s["x_hi_made"], k + 1)
                dve.tensor_tensor(x_lo[:, k, :], x[:, k, :], x_hi[:, k, :].bitcast(F32), ALU.subtract
                                  ).then_inc(s["x_lo_made"], 1)

            for k in range(KT):
                dve.wait_ge(s["wc_hi_made"], k + 1)
                if k == 0:
                    dve.wait_ge(s["quant"], KT)
                dve.scalar_tensor_tensor(out=wc_lo[:, k, :], in0=wc[k][:, :], scalar=1.0 / 15.0,
                                         in1=wc_hi[:, k, :].bitcast(F32), op0=ALU.mult, op1=ALU.subtract
                                         ).then_inc(s["wc_lo_made"], 1)

            for k in range(KT):
                dve.wait_ge(s["ad_hi_made"], k + 1)
                dve.tensor_tensor(ad_lo[:, k, :], ad_t[:, k, :], ad_hi[:, k, :].bitcast(F32), ALU.subtract
                                  ).then_inc(s["ad_lo_made"], 1)

            def x1_sum(i):
                n, m = i // KT, i % KT
                at = x[:, m, n * N:(n + 1) * N]
                dve.wait_ge(s["x1_done"], i + 1)
                dve.scalar_tensor_tensor(out=at, in0=bank[KT * n + m][:, :], scalar=bias0[:, m:m + 1], in1=at,
                                         op0=ALU.add, op1=ALU.add).then_inc(s["x1_made"], 1)

            def x1_low(i):
                n, m = i // KT, i % KT
                dve.wait_ge(s["x1_hi_made"], i + 1)
                dve.tensor_tensor(x1_lo[:, m, n * N:(n + 1) * N], x[:, m, n * N:(n + 1) * N],
                                  x1_hi[:, m, n * N:(n + 1) * N].bitcast(F32), ALU.subtract).then_inc(s["x1_lo_made"], 1)

            def low_mask(n):
                dve.wait_ge(s["low_done"], n + 1)
                if n:
                    dve.wait_ge(s["ad_mlo_made"], 1)
                mask = con[:, C_BM:C_BM + TG].unsqueeze(1).to_broadcast([P, 2, TG])
                dve.tensor_tensor(ad_m[:, :].rearrange("p (g t) -> p g t", g=2),
                                  bank[KT * n + 3][:, :].rearrange("p (g t) -> p g t", g=2), mask, ALU.mult
                                  ).then_inc(s["ad_m_made"], 1)
                dve.wait_ge(s["ad_mhi_made"], n + 1)
                dve.tensor_tensor(ad_mlo[:, :], ad_m[:, :], ad_mhi[:, :].bitcast(F32), ALU.subtract
                                  ).then_inc(s["ad_mlo_made"], 1)

            def c_low(i):
                n, m = i // KT, i % KT
                dve.wait_ge(s["c_hi_made"], i + 1)
                dve.scalar_tensor_tensor(out=c_lo[:, m, n * N:(n + 1) * N], in0=bank[KT * n + m][:, :],
                                         scalar=bias1[:, m:m + 1], in1=c_hi[:, m, n * N:(n + 1) * N].bitcast(F32),
                                         op0=ALU.add, op1=ALU.subtract).then_inc(s["c_lo_made"], 1)

            dve.wait_ge(bias_in, 32)
            for n in range(NH):
                for i in range(n * KT, (n + 1) * KT):
                    x1_sum(i)
                    if i % KT:
                        x1_low(i - 1)
                x1_low((n + 1) * KT - 1)
            low_mask(0)
            for m in range(KT):
                c_low(m)
            low_mask(1)

            def down_weights(u, parity, t):
                if not (isinstance(u, int) and u < 2):
                    dve.wait_ge(s["down_done"], u - 1)
                dve.tensor_copy(d_w[:, parity, :].unsqueeze(1), wd_raw[:, bass.ds(t, 1), :]).then_inc(s["d_w_made"], 1)

            for m in range(KT, 2 * KT):
                c_low(m)
            dve.wait_ge(down_in, 16)
            dve.wait_ge(s["c_done"], 2 * KT)

            def hidden(u, t, parity):
                dve.wait_ge(s["gact_made"], u + 1)
                dve.wait_ge(s["up_done"], u + 1)
                if not (isinstance(u, int) and u < 2):
                    dve.wait_ge(s["h_lo_made"], u - 1)
                dve.tensor_tensor(h[:, parity, :], gact[:, parity, :], bank[2 * parity + 1][:, :], ALU.mult
                                  ).then_inc(s["h_made"], 1)
                down_weights(u, parity, t)
                dve.wait_ge(s["h_hi_made"], u + 1)
                dve.tensor_tensor(h_lo[:, parity, :], h[:, parity, :], h_hi[:, parity, :].bitcast(F32), ALU.subtract
                                  ).then_inc(s["h_lo_made"], 1)

            def out_sum(n):
                for m in range(KT):
                    at = x[:, m, n * N:(n + 1) * N]
                    if m < KT - 1:
                        dve.wait_ge(s["sum_done"], (KT - 1) * n + m + 1)
                    else:
                        dve.wait_ge(s["down_done"], (n + 1) * MT)
                    dve.tensor_tensor(at, bank[KT + m][:, :], at, ALU.add).then_inc(s["out_made"], 1)

            for n in range(NH):
                base = n * MT
                hidden(base, 0, 0)
                if n:
                    out_sum(n - 1)
                hidden(base + 1, 1, 1)
                with dve.Fori(1, MT // 2) as i:
                    hidden(base + 2 * i, 2 * i, 0)
                    hidden(base + 2 * i + 1, 2 * i + 1, 1)
            out_sum(NH - 1)

        @block.tensor
        def _(pe):
            def keep_warm(count):
                for _ in range(count):
                    pe.matmul(bank[0][:, :], idle[:, 0:P], idle[:, :], start=True, stop=True)

            pe.wait_ge(s["idle_set"], 1)
            keep_warm(WARM_START)
            pe.wait_ge(lora_in, 32)
            for t in DELTA_ORDER:
                if t == DELTA_ORDER[2]:
                    pe.wait_ge(s["ones_set"], 1)
                    pe.wait_ge(s["place_made"], 1)
                    pe.matmul(bank[3][:, 0:2 * CODES], ones[:, :], place[:, :], start=True, stop=True
                              ).then_inc(s["jump_made"], 1)
                pe.matmul(delta[t][:, :], lora_b[:, t * P:(t + 1) * P], lora_a[:, :], start=True, stop=True
                          ).then_inc(s["delta_made"], 1)

            def turn(g, k):
                return pe.transpose(wc[k][:, g * P:(g + 1) * P], ad_raw[:, g, k * P:(k + 1) * P],
                                    con[:, C_ID:C_ID + P])

            pe.wait_ge(con_in, 16)
            pe.wait_ge(s["dsb_made"], KT)
            for g in range(NG - 1):
                pe.wait_ge(ad_in[g], 16)
                for k in range(KT):
                    turn(g, k)

            def add_jump(e, parity):
                pe.wait_ge(s["diag_made"], 2 * e + 2)
                for t in range(KT):
                    if t % 2 == 0:
                        pe.wait_ge(s["above_made"], 2 * e - 3 + t // 2)
                    for part in range(2):
                        mm = pe.matmul(acc[t][:, :], diag[:, parity, part, :], above[:, parity, t, :],
                                       start=False, stop=False, skip_group_check=True)
                    mm.then_inc(s["acc_used"], 1)

            pe.wait_ge(s["jump_read"], 1)
            for i, (e, t) in enumerate(FIRST):
                pe.wait_ge(s["diag_made"], 2 * e + 2)
                pe.wait_ge(s["above_first"], i + 1)
                for part in range(2):
                    mm = pe.matmul(acc[t][:, :], diag[:, e, part, :], above[:, e, t, :],
                                   start=(e == 0 and part == 0), stop=False, skip_group_check=True)
                mm.then_inc(s["acc_used"], 1)
            pe.wait_ge(ad_in[NG - 1], 16)
            for k in range(KT):
                turn(NG - 1, k).then_inc(s["adt_psum"], 1)
            pe.wait_ge(s["pairs_made"], 1)
            pairs = pe.value_load(npairs[0:1, 0:1], min_val=1, max_val=CODES // 2 - 1)
            with pe.Fori(0, pairs) as j:
                add_jump(2 * j + 2, 0)
                add_jump(2 * j + 3, 1)
            def three(dst, w_hi, w_lo, v_hi, v_lo, start, stop):
                pe.matmul(dst, w_hi, v_hi, start=start, stop=False)
                pe.matmul(dst, w_hi, v_lo, start=False, stop=False)
                return pe.matmul(dst, w_lo, v_hi, start=False, stop=stop)

            for t in range(KT):
                if t == 0:
                    pe.wait_ge(s["quant_first"], 1)
                    pe.wait_ge(s["w2t_made"], 1)
                else:
                    pe.wait_ge(s["w2t_lo_made"], t)
                    pe.wait_ge(s["w01_lo_made"], t)
                for k in range(KT):
                    at = slice(k * P, (k + 1) * P)
                    if t == 0:
                        pe.wait_ge(s["adt_made"], k + 1)
                        if k == KT // 2:
                            pe.wait_ge(s["quant"], 1)
                        pe.matmul(wc[k][:, :], w01[:, 0, at], w2t[:, 0, :], start=True, stop=False)
                    else:
                        mm = three(wc[k][:, :], w01_hi[:, t - 1, at], w01_lo[:, t - 1, at],
                                   w2t_hi[:, t - 1, :], w2t_lo[:, t - 1, :], False, t == KT - 1)
                    if t == KT - 1:
                        mm.then_inc(s["wc_done"], 1)

            pe.wait_ge(s["x_lo_made"], KT)
            for k in range(KT):
                pe.wait_ge(s["wc_hi_made"], k + 1)
                pe.wait_ge(s["wc_lo_made"], k + 1)
                for m in range(KT):
                    mm = three(bank[m][:, :], wc_hi[:, k, m * P:(m + 1) * P], wc_lo[:, k, m * P:(m + 1) * P],
                               x_hi[:, k, 0:N], x_lo[:, k, 0:N], k == 0, k == KT - 1)
                    if k == KT - 1:
                        mm.then_inc(s["x1_done"], 1)
            for m in range(KT):
                for k in range(KT):
                    mm = three(bank[KT + m][:, :], wc_hi[:, k, m * P:(m + 1) * P], wc_lo[:, k, m * P:(m + 1) * P],
                               x_hi[:, k, N:T], x_lo[:, k, N:T], k == 0, k == KT - 1)
                mm.then_inc(s["x1_done"], 1)

            for n in range(NH):
                pe.wait_ge(s["x1_lo_made"], (n + 1) * KT)
                for gg in range(2):
                    g = 2 * n + gg
                    for k in range(KT):
                        mm = three(bank[KT * n + 3][:, gg * TG:(gg + 1) * TG], ad_hi[:, k, g * P:(g + 1) * P],
                                   ad_lo[:, k, g * P:(g + 1) * P], x1_hi[:, k, g * TG:(g + 1) * TG],
                                   x1_lo[:, k, g * TG:(g + 1) * TG], k == 0, k == KT - 1)
                mm.then_inc(s["low_done"], 1)
                for m in range(KT):
                    if m == KT - 1:
                        pe.wait_ge(s["ad_m_made"], n + 1)
                    for k in range(KT):
                        three(bank[KT * n + m][:, :], w1_hi[:, k, m * P:(m + 1) * P], w1_lo[:, k, m * P:(m + 1) * P],
                              x1_hi[:, k, n * N:(n + 1) * N], x1_lo[:, k, n * N:(n + 1) * N], k == 0, False)
                    pe.wait_ge(s["ad_mlo_made"], n + 1)
                    for gg in range(2):
                        g = 2 * n + gg
                        mm = three(bank[KT * n + m][:, gg * TG:(gg + 1) * TG], bd_hi[:, g, m * P:(m + 1) * P],
                                   bd_lo[:, g, m * P:(m + 1) * P], ad_mhi[:, gg * TG:(gg + 1) * TG],
                                   ad_mlo[:, gg * TG:(gg + 1) * TG], False, gg == 1)
                    mm.then_inc(s["c_done"], 1)

            def gate_up(u, parity, n):
                tok = slice(n * N, (n + 1) * N)
                for part in range(2):
                    pe.wait_ge(s["gu_w_made"], 2 * u + part + 1)
                    if not (isinstance(u, int) and u < 2):
                        if part == 0:
                            pe.wait_ge(s["h_made"], u - 1)
                    for k in range(KT):
                        w = gu_w[:, parity, part, k, :]
                        pe.matmul(bank[2 * parity + part][:, :], w, c_hi[:, k, tok], start=(k == 0), stop=False)
                        mm = pe.matmul(bank[2 * parity + part][:, :], w, c_lo[:, k, tok], start=False,
                                       stop=(k == KT - 1))
                    mm.then_inc(s["up_done" if part else "gate_done"], 1)

            def down(u, parity, first=False, last=False):
                pe.wait_ge(s["d_w_made"], u + 1)
                pe.wait_ge(s["h_hi_made"], u + 1)
                pe.wait_ge(s["h_lo_made"], u + 1)
                for m in range(KT):
                    w = d_w[:, parity, m * P:(m + 1) * P]
                    pe.matmul(bank[KT + m][:, :], w, h_hi[:, parity, :], start=first, stop=False,
                              skip_group_check=True)
                    mm = pe.matmul(bank[KT + m][:, :], w, h_lo[:, parity, :], start=False, stop=last,
                                   skip_group_check=True)
                    if last and m < KT - 1:
                        mm.then_inc(s["sum_done"], 1)
                mm.then_inc(s["down_done"], 1)

            for n in range(NH):
                base = n * MT
                if n == 0:
                    pe.wait_ge(s["c_lo_made"], KT)
                    gate_up(0, 0, 0)
                gate_up(base + 1, 1, n)
                if n:
                    pe.wait_ge(s["out_made"], KT)
                else:
                    pe.wait_ge(s["c_lo_made"], 2 * KT)
                down(base, 0, first=True)
                with pe.Fori(1, MT // 2) as i:
                    gate_up(base + 2 * i, 0, n)
                    down(base + 2 * i - 1, 1)
                    gate_up(base + 2 * i + 1, 1, n)
                    down(base + 2 * i, 0)
                if n + 1 < NH:
                    gate_up(base + MT, 0, n + 1)
                down(base + MT - 1, 1, last=True)


def host_constants(np):
    con = np.zeros((P, C_N), np.float32)
    con[:, C_ID:C_ID + P] = np.eye(P)
    rows, toks = np.arange(P)[:, None], np.arange(TG)[None, :]
    con[:, C_BM:C_BM + TG] = np.where(rows // R1 == toks // TB, LORA1, 0.0)
    con[:CODES, C_TRI:C_TRI + CODES] = np.tril(np.ones((CODES, CODES)))
    con[:, C_IOTA:C_IOTA + CODES] = np.arange(1, CODES + 1)
    return con


def kernel(**inputs):
    import numpy as np
    import concourse.bacc as bacc
    from concourse import mybir as mb
    from concourse.bass_utils import run_bass_kernel_spmd as run

    v = {k: np.asarray(x) for k, x in inputs.items()}
    arrays = {
        "codebook": v["condB_codebook"].reshape(1, CODES),
        "slog": v["L0_cond_scale_log"].reshape(2, P, 2, CG).transpose(1, 0, 2, 3).reshape(P, KT * CG),
        "lora_a": v["L0_cond_lora_A"],
        "lora_b": v["L0_cond_lora_B"].reshape(2, P, 2, RANK0).transpose(3, 0, 2, 1).reshape(RANK0, D),
        "con": host_constants(np),
        "w0": v["L0_cond_weight"].reshape(2, P, 2, D).transpose(0, 2, 1, 3).reshape(KT, P, D),
        "slot": np.concatenate([np.repeat(v["itok_B_0_23"], R1).reshape(NG, P).T,
                                (np.arange(P, dtype=np.int32) % R1)[:, None]], axis=1),
        "q4": v["L0_ffn_weight_q4"].reshape(D, D // 2).T,
        "s2": v["L0_ffn_weight_scale"].reshape(D, D // GRP).T,
        "x": v["x"].reshape(T, D).T,
        "w1": v["L1_cond_W"].T,
        "bias0": v["L0_ffn_bias"].reshape(KT, P).T,
        "bias1": v["L1_cond_b"].reshape(KT, P).T,
        "lora1_a": v["L1_cond_lora_As"].transpose(0, 2, 1).reshape(SLOTS * R1, D),
        "lora1_b": v["L1_cond_lora_Bs"].reshape(SLOTS * R1, D),
        "wg": v["L1_ffn_W_gate"].T,
        "wu": v["L1_ffn_W_up"].T,
        "wd": v["L1_ffn_W_down"].T,
    }
    arrays = {k: np.ascontiguousarray(x) for k, x in arrays.items()}
    nc = bacc.Bacc("TRN2", target_bir_lowering=False, num_devices=1)
    aps = {k: nc.dram_tensor("in_" + k, x.shape, mb.dt.from_np(x.dtype), kind="ExternalInput").ap()
           for k, x in arrays.items()}
    out = nc.dram_tensor("out_t", (D, T), mb.dt.float32, kind="ExternalOutput").ap()
    build_program(nc, aps, out)
    got = run(nc, [{"in_" + k: x for k, x in arrays.items()}], core_ids=[0]).results[0]["out_t"]
    return np.ascontiguousarray(np.asarray(got).T).reshape(B, TB, D)
```

```python
from contextlib import ExitStack

import concourse.bass as bass
from concourse import mybir

F32 = mybir.dt.float32
F32R = mybir.dt.float32r
F16 = mybir.dt.float16
BF16 = mybir.dt.bfloat16
I32 = mybir.dt.int32
ALU = mybir.AluOpType
ACT = mybir.ActivationFunctionType
AX_X = mybir.AxisListType.X

P = 128
T = 1024
D = 512
KT = D // P
NH = 2
N = T // NH
CODES = 32
CG = 4
RANK0 = 64
LORA0 = 32.0 / 64.0
GRP = 32
WARM_START = 10
R1 = 16
LORA1 = 32.0 / 16.0
SLOTS = 32
B = 32
TB = T // B
GB = P // R1
NG = B // GB
TG = GB * TB
M = 1792
MT = M // P
LAST_STORES = ((0, 0, 2), (0, 2, 2), (1, 0, 2), (1, 2, 1), (1, 3, 1))
HALVES = (slice(0, N // 2), slice(N // 2, N))

C_ID = 0
C_BM = C_ID + P
C_TRI = C_BM + TG
C_IOTA = C_TRI + CODES
C_N = C_IOTA + CODES

DELTA_ORDER = (0, 3, 1, 2)
FIRST = ((0, 0), (1, 0), (0, 1), (0, 3), (1, 1), (1, 3), (0, 2), (1, 2))
FIRST_OF_0 = 7


def build_program(nc, a, out):
    ctx = ExitStack()
    with ctx:
        def sb(name, shape, dt, stack=ctx):
            return stack.enter_context(nc.sbuf_tensor(name, shape, dt))

        def sem(name):
            return ctx.enter_context(nc.semaphore(name))

        con = sb("con", [P, C_N], F32)
        ones = sb("ones", [CODES, P], F32)
        codes_in = sb("codes_in", [P, CODES], F32)
        half = sb("half", [P, CODES], F32)
        code = sb("code", [P, CODES], F32)
        absc = sb("absc", [P, CODES], F32)
        peak = sb("peak", [P, 1], F32)
        rpeak = sb("rpeak", [P, 1], F32)
        step = sb("step", [P, CODES], F32)
        bound = sb("bound", [P, CODES + 1], F32)
        fresh = sb("fresh", [P, CODES], F32)
        fbound = sb("fbound", [P, CODES], F32)
        pick = sb("pick", [CODES, 3, CODES], F32)
        rank = sb("rank", [CODES, 1], F32)
        step_c = sb("step_c", [CODES, 1], F32)
        bound_c = sb("bound_c", [CODES, 1], F32)
        place = sb("place", [CODES, 2 * CODES], F32)
        jump = sb("jump", [P, 2 * CODES], F32)
        jump_hi = sb("jump_hi", [P, CODES], F32R)
        jump_lo = sb("jump_lo", [P, CODES], F32)
        njump = sb("njump", [P, 1], I32)
        npairs = sb("npairs", [P, 1], I32)
        diag = sb("diag", [P, 2, 2, P], F32R)
        slog = sb("slog", [P, KT * CG], F32)
        scale = sb("scale", [P, KT * CG], F32)
        rscale = sb("rscale", [P, KT * CG], F32)
        bias0 = sb("bias0", [P, KT], F32)
        bias1 = sb("bias1", [P, KT], F32)
        slot = sb("slot", [P, NG + 1], I32)
        spare = sb("spare", [CODES, 2], F32)
        row16 = sb("row16", [P, NG], I32)
        row = sb("row", [P, NG], I32)
        x = sb("x", [P, KT, T], F32)
        wg_raw = sb("wg_raw", [P, KT, M], F16)
        wu_raw = sb("wu_raw", [P, KT, M], F16)
        w1_hi = sb("w1_hi", [P, KT, D], F32R)
        w1_lo = sb("w1_lo", [P, KT, D], F32R)
        bd_hi = sb("bd_hi", [P, NG, D], F32R)
        bd_lo = sb("bd_lo", [P, NG, D], F32R)

        def zone(name, size, *uses):
            got = []
            for use in uses:
                with ExitStack() as part:
                    got.append([sb(n, s, d, part) for n, s, d in use])
            sb(name, [P, size], F32)
            return got

        (w2t_hi, w2t_lo), (ad_m, ad_mhi, ad_mlo) = zone(
            "zone_w2t", 2 * (KT - 1) * D,
            [("w2t_hi", [P, KT - 1, D], F32R), ("w2t_lo", [P, KT - 1, D], F32R)],
            [("ad_m", [P, 2 * TG], F32), ("ad_mhi", [P, 2 * TG], F32R), ("ad_mlo", [P, 2 * TG], F32R)])
        (above,), (w01_hi, w01_lo), (ad_hi, ad_lo) = zone(
            "zone_above", 2 * KT * D,
            [("above", [P, 2, KT, D], F32R)],
            [("w01_hi", [P, KT - 1, D], F32R), ("w01_lo", [P, KT - 1, D], F32R)],
            [("ad_hi", [P, KT, D], F32R), ("ad_lo", [P, KT, D], F32R)])
        (w0, q, w2t, dsb), (w01,), (wc_hi, wc_lo, wd_raw), (gu_w, d_w) = zone(
            "zone_l0", 4 * KT * D,
            [("w0", [P, KT, D], F32), ("q", [P, KT, D], F32), ("w2t", [P, KT, D], F32), ("dsb", [P, KT, D], F32)],
            [("w01", [P, KT, D], F32)],
            [("wc_hi", [P, KT, D], F32R), ("wc_lo", [P, KT, D], F32R), ("wd_raw", [P, MT, D], F16)],
            [("gu_w", [P, 2, 2, KT, P], F32R), ("d_w", [P, 2, D], F32R)])
        (lora, idle, _, q4, s2, lev), (x_hi, x_lo), (c_hi, c_lo) = zone(
            "zone_x", 2 * KT * T,
            [("lora", [RANK0, 2 * D], F32), ("idle", [P, N], BF16),
             ("beside_x_hi", [P, KT * T - 2 * D - N // 2], F32),
             ("q4", [P, 2, D], I32), ("s2", [P, 2, D], F32), ("lev", [P, KT, D], I32)],
            [("x_hi", [P, KT, T], F32R), ("x_lo", [P, KT, T], F32R)],
            [("c_hi", [P, KT, T], F32R), ("c_lo", [P, KT, T], F32R)])
        ((w1_raw, ad_raw, bd_raw, ad_t), (x1_hi, x1_lo), (h, h_hi, h_lo, gact)) = zone(
            "zone_x1", 2 * KT * T,
            [("w1_raw", [P, KT, D], F32), ("ad_raw", [P, NG, D], F32), ("bd_raw", [P, NG, D], F32),
             ("ad_t", [P, KT, D], F32)],
            [("x1_hi", [P, KT, T], F32R), ("x1_lo", [P, KT, T], F32R)],
            [("h", [P, 2, N], F32), ("h_hi", [P, 2, N], F32R), ("h_lo", [P, 2, N], F32R),
             ("gact", [P, 2, N], F32)])

        bank = [ctx.enter_context(nc.psum_tensor(f"bank{i}", [P, N], F32)) for i in range(8)]
        acc, delta, wc = bank[0:4], bank[4:8], bank[4:8]

        codes_in_ready, con_in, slog_in, lora_in, q4_in, s2_in = (sem(n) for n in (
            "codes_in_ready", "con_in", "slog_in", "lora_in", "q4_in", "s2_in"))
        w0_in = [sem(f"w0_in{i}") for i in range(KT)]
        x_in = [sem(f"x_in{i}") for i in range(KT)]
        w1_in, slot_in, bias_in, gate_up_in, down_in = (sem(n) for n in (
            "w1_in", "slot_in", "bias_in", "gate_up_in", "down_in"))
        ad_in = [sem(f"ad_in{i}") for i in range(NG)]
        bd_in = [sem(f"bd_in{i}") for i in range(NG)]
        stored = sem("stored")
        names = ("tiny", "ones_set", "idle_set", "sum_done", "last_done", "scale_made", "rscale_made",
                 "delta_made", "dsb_made", "q_sum", "q_made", "above_first", "above_made", "diag_made",
                 "acc_used", "place_made", "jump_made", "levels", "levels_used", "w2t_made", "quant",
                 "quant_first", "w01_hi_made", "w01_lo_made", "w2t_hi_made", "w2t_lo_made", "row_made",
                 "adt_psum", "adt_made", "x_hi_made", "x_lo_made", "w1_hi_made", "w1_lo_made", "bd_hi_made",
                 "bd_lo_made", "ad_hi_made", "ad_lo_made", "wc_done", "wc_hi_made", "wc_lo_made", "x1_done",
                 "x1_made", "x1_hi_made", "x1_lo_made", "low_done", "ad_m_made", "ad_mhi_made", "ad_mlo_made",
                 "c_done", "c_hi_made", "c_lo_made", "gu_w_made", "d_w_made", "gate_done", "up_done",
                 "gact_made", "h_made", "h_hi_made", "h_lo_made", "down_done", "out_made", "jump_read",
                 "split_made", "pairs_made")
        s = {n: sem(n) for n in names}

        block = ctx.enter_context(nc.Block())

        @block.sync
        def _(sp):
            sp.dma_start(codes_in[:, :], a["codebook"].to_broadcast([P, CODES])).then_inc(codes_in_ready, 16)
            sp.dma_start(lora[:, :], a["lora"]).then_inc(lora_in, 16)
            sp.dma_start(w0[:, 0, :], a["w0"][0]).then_inc(w0_in[0], 16)
            sp.dma_start(con[:, :], a["con"]).then_inc(con_in, 16)
            for t in DELTA_ORDER[1:]:
                sp.dma_start(w0[:, t, :], a["w0"][t]).then_inc(w0_in[t], 16)
            sp.wait_ge(ad_in[0], 16)
            sp.wait_ge(ad_in[1], 16)
            sp.dma_start(q4[:, :, :], a["q4"].rearrange("(w p) n -> p w n", p=P)).then_inc(q4_in, 16)
            for w in range(2):
                src = a["s2"][w * 8:(w + 1) * 8, :].unsqueeze(1).to_broadcast([8, 16, D])
                sp.dma_start(s2[:, w, :], src).then_inc(s2_in, 16)
            for k in range(KT):
                sp.dma_start(x[:, k, :], a["x"][k * P:(k + 1) * P, :]).then_inc(x_in[k], 16)
            sp.dma_start(w1_raw[:, :, :], a["w1"].rearrange("(k p) n -> p k n", p=P)).then_inc(w1_in, 16)
            sp.dma_start(bias0[:, :], a["bias0"]).then_inc(bias_in, 16)
            sp.dma_start(bias1[:, :], a["bias1"]).then_inc(bias_in, 16)
            for g in range(NG):
                sp.wait_ge(bd_in[g], 16)
            sp.dma_start(wg_raw[:, :, :], a["wg"].rearrange("(k p) m -> p k m", p=P)).then_inc(gate_up_in, 16)
            sp.dma_start(wu_raw[:, :, :], a["wu"].rearrange("(k p) m -> p k m", p=P)).then_inc(gate_up_in, 16)
            sp.wait_ge(s["wc_done"], KT)
            sp.dma_start(wd_raw[:, :, :], a["wd"].rearrange("(t p) n -> p t n", p=P)).then_inc(down_in, 16)
            for m in range(KT):
                sp.wait_ge(s["out_made"], m + 1)
                sp.dma_start(out[m * P:(m + 1) * P, 0:N], x[:, m, 0:N]).then_inc(stored, 16)
            for i, m, count in LAST_STORES:
                sp.wait_ge(s["out_made"], KT + KT * i + m + count)
                at = slice(N + HALVES[i].start, N + HALVES[i].stop)
                sp.dma_start(out[m * P:(m + count) * P, at].rearrange("(m p) n -> p m n", p=P),
                             x[:, m:m + count, at]).then_inc(stored, 16)
            sp.wait_ge(stored, 16 * (KT + len(LAST_STORES)))

        @block.gpsimd
        def _(pool):
            pool.wait_ge(slot_in, 16)
            pool.tensor_scalar(row16[:, :], slot[:, 0:NG], float(R1), 0.0, ALU.mult, ALU.add).then_inc(s["row_made"], 1)
            pool.wait_ge(s["row_made"], 1)
            pool.tensor_tensor(row[:, :], row16[:, :], slot[:, NG:NG + 1].to_broadcast([P, NG]), ALU.add
                               ).then_inc(s["row_made"], 1)
            pool.wait_ge(s["row_made"], 2)
            for g in range(NG):
                pool.indirect_dma_start(ad_raw[:, g, :], None, a["lora1_a"],
                                        bass.IndirectOffsetOnAxis(ap=row[:, g:g + 1], axis=0)).then_inc(ad_in[g], 16)
            for i, t in enumerate((3, 2)):
                pool.wait_ge(w0_in[t], 16)
                pool.wait_ge(s["dsb_made"], DELTA_ORDER.index(t) + 1)
                pool.tensor_tensor(q[:, t, :], w0[:, t, :], dsb[:, t, :], ALU.add).then_inc(s["q_sum"], 1)
                pool.wait_ge(s["q_sum"], i + 1)
                pool.wait_ge(s["rscale_made"], 1)
                q3 = q[:, t, :].rearrange("p (g n) -> p g n", g=CG)
                rs = rscale[:, t * CG:(t + 1) * CG].unsqueeze(2).to_broadcast([P, CG, P])
                pool.tensor_tensor(q3, q3, rs, ALU.mult).then_inc(s["q_made"], 1)
            pool.wait_ge(s2_in, 32)

            def w2t_low(t):
                pool.wait_ge(s["w2t_hi_made"], t)
                pool.tensor_tensor(w2t_lo[:, t - 1, :], w2t[:, t, :], w2t_hi[:, t - 1, :].bitcast(F32), ALU.subtract
                                   ).then_inc(s["w2t_lo_made"], 1)

            for t in range(KT):
                pool.wait_ge(s["levels"], t + 1)
                pool.tensor_scalar(w2t[:, t, :], lev[:, t, :], 2.0, -15.0, ALU.mult, ALU.add
                                   ).then_inc(s["levels_used"], 1)
                pool.wait_ge(s["levels_used"], t + 1)
                pool.tensor_tensor(w2t[:, t, :], w2t[:, t, :], s2[:, t // 2, :], ALU.mult).then_inc(s["w2t_made"], 1)
                if t > 1:
                    w2t_low(t - 1)
            w2t_low(KT - 1)
            for g in range(NG):
                pool.indirect_dma_start(bd_raw[:, g, :], None, a["lora1_b"],
                                        bass.IndirectOffsetOnAxis(ap=row[:, g:g + 1], axis=0)).then_inc(bd_in[g], 16)
            for k in range(KT):
                pool.wait_ge(s["w1_hi_made"], k + 1)
                pool.tensor_tensor(w1_lo[:, k, :], w1_raw[:, k, :], w1_hi[:, k, :].bitcast(F32), ALU.subtract
                                   ).then_inc(s["w1_lo_made"], 1)
            for g in range(NG):
                pool.wait_ge(s["bd_hi_made"], g + 1)
                pool.tensor_tensor(bd_lo[:, g, :], bd_raw[:, g, :], bd_hi[:, g, :].bitcast(F32), ALU.subtract
                                   ).then_inc(s["bd_lo_made"], 1)

        @block.scalar
        def _(act):
            act.dma_start(slot[:, :], a["slot"]).then_inc(slot_in, 16)
            act.dma_start(slog[:, :], a["slog"]).then_inc(slog_in, 16)
            act.wait_ge(s["ones_set"], 1)
            act.activation(spare[:, 0:1], ones[:, 0:1], ACT.Exp)
            act.wait_ge(slog_in, 16)
            act.activation(scale[:, :], slog[:, :], ACT.Exp).then_inc(s["scale_made"], 1)

            def diagonal_part(i, col, parity):
                src, at = (jump, col + CODES) if i == 0 else (jump_lo, col)
                act.activation(diag[:, parity, i, :], con[:, C_ID:C_ID + P], ACT.Copy,
                               scale=src[:, bass.ds(at, 1)]).then_inc(s["diag_made"], 1)

            def diagonal(e, col, parity):
                act.wait_ge(s["acc_used"], KT * (e - 1))
                diagonal_part(0, col, parity)
                diagonal_part(1, col, parity)

            def lora_scaled(i):
                act.wait_ge(s["delta_made"], i + 1)
                act.activation(dsb[:, DELTA_ORDER[i], :], delta[DELTA_ORDER[i]][:, :], ACT.Copy, scale=LORA0
                               ).then_inc(s["dsb_made"], 1)

            lora_scaled(0)
            lora_scaled(1)
            act.wait_ge(con_in, 16)
            act.wait_ge(s["jump_read"], 1)
            diagonal_part(0, 0, 0)
            lora_scaled(2)
            act.wait_ge(s["split_made"], 1)
            diagonal_part(1, 0, 0)
            diagonal_part(0, 1, 1)
            diagonal_part(1, 1, 1)
            lora_scaled(3)
            act.wait_ge(s["pairs_made"], 2)
            pairs = act.value_load(npairs[0:1, 0:1], min_val=1, max_val=CODES // 2 - 1)
            act.wait_ge(s["acc_used"], FIRST_OF_0)
            with act.Fori(0, pairs) as j:
                diagonal(2 * j + 2, 2 * j + 2, 0)
                diagonal(2 * j + 3, 2 * j + 3, 1)
            for k in range(KT):
                act.wait_ge(s["adt_psum"], k + 1)
                act.activation(ad_t[:, k, :], wc[k][:, :], ACT.Copy).then_inc(s["adt_made"], 1)

            def x_high(k):
                act.wait_ge(x_in[k], 16)
                act.activation(x_hi[:, k, :], x[:, k, :], ACT.Copy).then_inc(s["x_hi_made"], 1)

            act.wait_ge(s["acc_used"], KT * (2 * pairs + 2))
            for t in range(1, KT):
                act.wait_ge(s["w2t_made"], t + 1)
                act.activation(w2t_hi[:, t - 1, :], w2t[:, t, :], ACT.Copy).then_inc(s["w2t_hi_made"], 1)
                act.wait_ge(s["quant"], t + 1)
                act.activation(w01_hi[:, t - 1, :], w01[:, t, :], ACT.Copy).then_inc(s["w01_hi_made"], 1)
                act.wait_ge(s["delta_made"], KT)
                x_high(t - 1)
            x_high(KT - 1)
            for k in range(KT):
                act.wait_ge(s["wc_done"], k + 1)
                act.wait_ge(s["w01_lo_made"], KT - 1)
                act.activation(wc_hi[:, k, :], wc[k][:, :], ACT.Copy, scale=1.0 / 15.0).then_inc(s["wc_hi_made"], 1)
            act.wait_ge(w1_in, 16)
            for k in range(KT):
                act.activation(w1_hi[:, k, :], w1_raw[:, k, :], ACT.Copy).then_inc(s["w1_hi_made"], 1)
            for g in range(NG):
                act.wait_ge(bd_in[g], 16)
                act.activation(bd_hi[:, g, :], bd_raw[:, g, :], ACT.Copy).then_inc(s["bd_hi_made"], 1)
            for k in range(KT):
                act.wait_ge(s["adt_made"], k + 1)
                act.activation(ad_hi[:, k, :], ad_t[:, k, :], ACT.Copy).then_inc(s["ad_hi_made"], 1)
            act.activation(spare[:, 1:2], ones[:, 0:1], ACT.Silu)
            act.wait_ge(s["w1_lo_made"], KT)
            act.wait_ge(s["ad_lo_made"], KT)
            act.wait_ge(s["bd_lo_made"], NG)

            def x1_high(i):
                n, m = i // KT, i % KT
                act.wait_ge(s["x1_made"], i + 1)
                act.activation(x1_hi[:, m, n * N:(n + 1) * N], x[:, m, n * N:(n + 1) * N], ACT.Copy
                               ).then_inc(s["x1_hi_made"], 1)

            def low_high(n):
                act.wait_ge(s["ad_m_made"], n + 1)
                if n:
                    act.wait_ge(s["c_done"], KT)
                act.activation(ad_mhi[:, :], ad_m[:, :], ACT.Copy).then_inc(s["ad_mhi_made"], 1)

            def c_high(i):
                n, m = i // KT, i % KT
                act.wait_ge(s["c_done"], i + 1)
                act.activation(c_hi[:, m, n * N:(n + 1) * N], bank[KT * n + m][:, :], ACT.Identity,
                               bias=bias1[:, m:m + 1]).then_inc(s["c_hi_made"], 1)

            for i in range(NH * KT):
                x1_high(i)
            low_high(0)
            act.wait_ge(bias_in, 32)
            for m in range(KT):
                c_high(m)
            low_high(1)
            act.wait_ge(gate_up_in, 32)

            def gate_weights(u, parity, col, first=False):
                if not first:
                    act.wait_ge(s["gate_done"], u - 1)
                act.activation(gu_w[:, parity, 0, :, :], wg_raw[:, :, bass.ds(col, P)], ACT.Copy
                               ).then_inc(s["gu_w_made"], 1)

            def up_weights(u, parity, col, first=False):
                if not first:
                    act.wait_ge(s["up_done"], u - 1)
                act.activation(gu_w[:, parity, 1, :, :], wu_raw[:, :, bass.ds(col, P)], ACT.Copy
                               ).then_inc(s["gu_w_made"], 1)

            for u in range(2):
                gate_weights(u, u, u * P, True)
                up_weights(u, u, u * P, True)
            for m in range(KT, 2 * KT):
                c_high(m)

            def hidden_last(u, parity):
                act.wait_ge(s["h_made"], u - 1)
                act.wait_ge(s["down_done"], u - 1)
                for i, tok in enumerate(HALVES):
                    act.wait_ge(s["gate_done"], u + 1 + i)
                    act.activation(gact[:, parity, tok], bank[2 - 2 * i][:, tok], ACT.Silu
                                   ).then_inc(s["gact_made"], 1)
                    act.wait_ge(s["h_made"], u + 1 + i)
                    act.activation(h_hi[:, parity, tok], h[:, parity, tok], ACT.Copy).then_inc(s["h_hi_made"], 1)

            def hidden(u, col2, parity, more=True):
                act.wait_ge(s["gate_done"], u + 1)
                if not (isinstance(u, int) and u < 2):
                    act.wait_ge(s["h_made"], u - 1)
                act.activation(gact[:, parity, :], bank[2 * parity][:, :], ACT.Silu).then_inc(s["gact_made"], 1)
                if more:
                    gate_weights(u + 2, parity, col2)
                act.wait_ge(s["h_made"], u + 1)
                if not (isinstance(u, int) and u < 2):
                    act.wait_ge(s["down_done"], u - 1)
                act.activation(h_hi[:, parity, :], h[:, parity, :], ACT.Copy).then_inc(s["h_hi_made"], 1)
                if more:
                    up_weights(u + 2, parity, col2)

            act.wait_ge(s["c_done"], 2 * KT)
            for n in range(NH):
                base = n * MT
                hidden(base, 2 * P, 0)
                hidden(base + 1, 3 * P, 1)
                with act.Fori(1, MT // 2 - 1) as i:
                    hidden(base + 2 * i, i * (2 * P) + 2 * P, 0)
                    hidden(base + 2 * i + 1, i * (2 * P) + 3 * P, 1)
                hidden(base + MT - 2, 0, 0, n == 0)
                if n == 0:
                    hidden(base + MT - 1, P, 1)
                else:
                    hidden_last(base + MT - 1, 1)

        @block.vector
        def _(dve):
            steps = [0]

            def mark(ins):
                steps[0] += 1
                ins.then_inc(s["tiny"], 1)
                return steps[0]

            def after(number):
                dve.wait_ge(s["tiny"], number)

            def link(ins):
                after(mark(ins))

            dve.memset(idle[:, :], 0.0).then_inc(s["idle_set"], 1)
            dve.memset(ones[:, :], 1.0).then_inc(s["ones_set"], 1)
            dve.memset(bound[:, 0:1], -2.0)
            dve.memset(bound[:, CODES:CODES + 1], 2.0)
            dve.memset(step[:, CODES - 1:CODES], 0.0)
            link(dve.memset(fresh[:, CODES - 1:CODES], 0.0))
            dve.wait_ge(codes_in_ready, 16)
            link(dve.scalar_tensor_tensor(out=absc[:, :], in0=codes_in[:, :], scalar=-1.0, in1=codes_in[:, :],
                                          op0=ALU.mult, op1=ALU.max))
            link(dve.tensor_reduce(peak[:, :], absc[:, :], AX_X, ALU.max))
            link(dve.tensor_scalar(peak[:, :], peak[:, :], 1e-8, None, ALU.max))
            link(dve.reciprocal(rpeak[:, :], peak[:, :]))
            half_made = mark(dve.tensor_scalar(half[:, :], codes_in[:, :], rpeak[:, 0:1], 0.5, ALU.mult, ALU.mult))
            code_made = mark(dve.tensor_scalar(code[:, :], codes_in[:, :], rpeak[:, 0:1], None, ALU.mult))
            after(half_made)
            bound_made = mark(dve.tensor_tensor(bound[:, 1:CODES], half[:, 0:CODES - 1], half[:, 1:CODES], ALU.add))
            after(code_made)
            step_made = mark(dve.tensor_tensor(step[:, 0:CODES - 1], code[:, 1:CODES], code[:, 0:CODES - 1],
                                               ALU.subtract))
            after(bound_made)
            root = bound[:, CODES // 2:CODES // 2 + 1]
            left, right = (bound[:, i:i + 1] for i in (CODES // 4, 3 * CODES // 4))
            dve.tensor_tensor(left, left, root, ALU.min)
            link(dve.tensor_tensor(right, right, root, ALU.max))
            d = CODES // 8
            while d:
                mid = bound[:, d:CODES:2 * d]
                link(dve.tensor_tensor(mid, mid, bound[:, 0:CODES - d:2 * d], ALU.max))
                link(dve.tensor_tensor(mid, mid, bound[:, 2 * d:CODES + 1:2 * d], ALU.min))
                d //= 2
            fresh_made = mark(dve.tensor_tensor(fresh[:, 0:CODES - 1], bound[:, 1:CODES], bound[:, 0:CODES - 1],
                                                ALU.is_gt))
            dve.wait_ge(s["scale_made"], 1)
            dve.reciprocal(rscale[:, :], scale[:, :]).then_inc(s["rscale_made"], 1)
            after(fresh_made)
            fbound_made = mark(dve.tensor_tensor(fbound[:, :], bound[:, 1:CODES + 1], fresh[:, :], ALU.mult))
            count_made = mark(dve.tensor_reduce(peak[:, :], fresh[:, :], AX_X, ALU.add))
            dve.wait_ge(con_in, 16)

            def diagonal_sum(col, i, src, mask):
                return dve.scalar_tensor_tensor(out=pick[:, i, :], in0=src[0:CODES, :], scalar=1.0,
                                                in1=con[0:CODES, mask:mask + CODES], op0=ALU.mult, op1=ALU.mult,
                                                accum_out=col[:, :])

            diagonal_sum(rank, 0, fresh, C_TRI)
            after(step_made)
            diagonal_sum(step_c, 1, step, C_ID)
            after(fbound_made)
            picked = mark(diagonal_sum(bound_c, 2, fbound, C_ID))
            after(count_made)
            dve.tensor_scalar(njump[:, :], peak[:, :], -1.0, 2.0, ALU.add, ALU.max).then_inc(s["pairs_made"], 1)
            after(picked)
            iota = con[0:CODES, C_IOTA:C_IOTA + CODES]
            dve.tensor_scalar(place[:, 0:CODES], iota, rank[:, 0:1], bound_c[:, 0:1], ALU.is_equal, ALU.mult)
            dve.tensor_scalar(place[:, CODES:2 * CODES], iota, rank[:, 0:1], step_c[:, 0:1], ALU.is_equal,
                              ALU.mult).then_inc(s["place_made"], 1)
            dve.wait_ge(s["pairs_made"], 1)
            dve.tensor_scalar(npairs[:, :], njump[:, :], 1, None, ALU.logical_shift_right).then_inc(s["pairs_made"], 1)

            def add_lora(t):
                dve.wait_ge(w0_in[t], 16)
                dve.wait_ge(s["dsb_made"], DELTA_ORDER.index(t) + 1)
                return dve.tensor_tensor(q[:, t, :], w0[:, t, :], dsb[:, t, :], ALU.add)

            def by_scale(t):
                rs = rscale[:, t * CG:(t + 1) * CG].unsqueeze(2).to_broadcast([P, CG, P])
                q3 = q[:, t, :].rearrange("p (g n) -> p g n", g=CG)
                return dve.tensor_tensor(q3, q3, rs, ALU.mult)

            added = mark(add_lora(0))
            dve.wait_ge(s["jump_made"], 1)
            dve.tensor_copy(jump[:, :], bank[3][:, 0:2 * CODES]).then_inc(s["jump_read"], 1)
            dve.wait_ge(s["jump_read"], 1)
            high = mark(dve.tensor_copy(jump_hi[:, :], jump[:, CODES:2 * CODES]))
            dve.wait_ge(s["rscale_made"], 1)
            after(added)
            scaled = mark(by_scale(0))
            after(high)
            dve.tensor_tensor(jump_lo[:, :], jump[:, CODES:2 * CODES], jump_hi[:, :].bitcast(F32), ALU.subtract
                              ).then_inc(s["split_made"], 1)
            after(scaled)
            for e, t in FIRST:
                if (e, t) == (0, 1):
                    link(add_lora(1))
                    link(by_scale(1))
                elif e == 0 and t > 1:
                    dve.wait_ge(s["q_made"], 4 - t)
                dve.tensor_scalar(above[:, e, t, :], q[:, t, :], jump[:, e:e + 1], None, ALU.is_gt
                                  ).then_inc(s["above_first"], 1)

            def compare(e, col, parity):
                dve.wait_ge(s["acc_used"], KT * (e - 1))
                for half_ in range(2):
                    two = slice(2 * half_, 2 * half_ + 2)
                    dve.tensor_scalar(above[:, parity, two, :], q[:, two, :], jump[:, bass.ds(col, 1)], None,
                                      ALU.is_gt).then_inc(s["above_made"], 1)

            def level(t):
                w, high = t // 2, t % 2
                if high:
                    dve.tensor_scalar(lev[:, t, :], q4[:, w, :], 4, 15, ALU.logical_shift_right,
                                      ALU.bitwise_and).then_inc(s["levels"], 1)
                else:
                    dve.tensor_scalar(lev[:, t, :], q4[:, w, :], 15, None, ALU.bitwise_and
                                      ).then_inc(s["levels"], 1)

            dve.wait_ge(s["pairs_made"], 2)
            pairs = dve.value_load(npairs[0:1, 0:1], min_val=1, max_val=CODES // 2 - 1)
            dve.wait_ge(q4_in, 16)
            level(0)
            level(1)
            dve.wait_ge(s["acc_used"], FIRST_OF_0)
            with dve.Fori(0, pairs) as j:
                compare(2 * j + 2, 2 * j + 2, 0)
                compare(2 * j + 3, 2 * j + 3, 1)
            level(2)
            level(3)

            def w01_low(t):
                dve.wait_ge(s["w01_hi_made"], t)
                dve.tensor_tensor(w01_lo[:, t - 1, :], w01[:, t, :], w01_hi[:, t - 1, :].bitcast(F32), ALU.subtract
                                  ).then_inc(s["w01_lo_made"], 1)

            def coded(t, groups):
                dve.wait_ge(s["acc_used"], KT * (2 * pairs + 1) + t + 1)
                n = groups.stop - groups.start
                at = slice(groups.start * P, groups.stop * P)
                sc = scale[:, t * CG + groups.start:t * CG + groups.stop].unsqueeze(2).to_broadcast([P, n, P])
                return mark(dve.scalar_tensor_tensor(out=w01[:, t, at].rearrange("p (g n) -> p g n", g=n),
                                                     in0=acc[t][:, at].rearrange("p (g n) -> p g n", g=n),
                                                     scalar=code[:, 0:1], in1=sc, op0=ALU.add, op1=ALU.mult))

            def with_lora(t, groups, number):
                after(number)
                at = slice(groups.start * P, groups.stop * P)
                return dve.tensor_tensor(w01[:, t, at], w01[:, t, at], dsb[:, t, at], ALU.add)

            def x_low(k):
                dve.wait_ge(s["x_hi_made"], k + 1)
                dve.tensor_tensor(x_lo[:, k, :], x[:, k, :], x_hi[:, k, :].bitcast(F32), ALU.subtract
                                  ).then_inc(s["x_lo_made"], 1)

            some, rest, every = slice(0, CG // 2), slice(CG // 2, CG), slice(0, CG)
            with_lora(0, some, coded(0, some)).then_inc(s["quant_first"], 1)
            number = coded(0, rest)
            number1 = coded(1, every)
            with_lora(0, rest, number).then_inc(s["quant"], 1)
            with_lora(1, every, number1).then_inc(s["quant"], 1)
            for t in range(2, KT):
                number = coded(t, every)
                w01_low(t - 1)
                with_lora(t, every, number).then_inc(s["quant"], 1)
            dve.wait_ge(s["w2t_made"], KT)
            x_low(0)
            w01_low(KT - 1)
            x_low(1)

            for k in range(KT):
                dve.wait_ge(s["wc_hi_made"], k + 1)
                if k == 0:
                    dve.wait_ge(s["quant"], KT)
                dve.scalar_tensor_tensor(out=wc_lo[:, k, :], in0=wc[k][:, :], scalar=1.0 / 15.0,
                                         in1=wc_hi[:, k, :].bitcast(F32), op0=ALU.mult, op1=ALU.subtract
                                         ).then_inc(s["wc_lo_made"], 1)
                if k + 2 < KT:
                    x_low(k + 2)

            for k in range(KT):
                dve.wait_ge(s["ad_hi_made"], k + 1)
                dve.tensor_tensor(ad_lo[:, k, :], ad_t[:, k, :], ad_hi[:, k, :].bitcast(F32), ALU.subtract
                                  ).then_inc(s["ad_lo_made"], 1)

            def x1_sum(i):
                n, m = i // KT, i % KT
                at = x[:, m, n * N:(n + 1) * N]
                dve.wait_ge(s["x1_done"], i + 1)
                dve.scalar_tensor_tensor(out=at, in0=bank[KT * n + m][:, :], scalar=bias0[:, m:m + 1], in1=at,
                                         op0=ALU.add, op1=ALU.add).then_inc(s["x1_made"], 1)

            def x1_low(i):
                n, m = i // KT, i % KT
                dve.wait_ge(s["x1_hi_made"], i + 1)
                dve.tensor_tensor(x1_lo[:, m, n * N:(n + 1) * N], x[:, m, n * N:(n + 1) * N],
                                  x1_hi[:, m, n * N:(n + 1) * N].bitcast(F32), ALU.subtract).then_inc(s["x1_lo_made"], 1)

            def low_mask(n):
                dve.wait_ge(s["low_done"], n + 1)
                if n:
                    dve.wait_ge(s["ad_mlo_made"], 1)
                mask = con[:, C_BM:C_BM + TG].unsqueeze(1).to_broadcast([P, 2, TG])
                dve.tensor_tensor(ad_m[:, :].rearrange("p (g t) -> p g t", g=2),
                                  bank[KT * n + 3][:, :].rearrange("p (g t) -> p g t", g=2), mask, ALU.mult
                                  ).then_inc(s["ad_m_made"], 1)
                dve.wait_ge(s["ad_mhi_made"], n + 1)
                dve.tensor_tensor(ad_mlo[:, :], ad_m[:, :], ad_mhi[:, :].bitcast(F32), ALU.subtract
                                  ).then_inc(s["ad_mlo_made"], 1)

            def c_low(i):
                n, m = i // KT, i % KT
                dve.wait_ge(s["c_hi_made"], i + 1)
                dve.scalar_tensor_tensor(out=c_lo[:, m, n * N:(n + 1) * N], in0=bank[KT * n + m][:, :],
                                         scalar=bias1[:, m:m + 1], in1=c_hi[:, m, n * N:(n + 1) * N].bitcast(F32),
                                         op0=ALU.add, op1=ALU.subtract).then_inc(s["c_lo_made"], 1)

            dve.wait_ge(bias_in, 32)
            for n in range(NH):
                for i in range(n * KT, (n + 1) * KT):
                    x1_sum(i)
                    if i % KT:
                        x1_low(i - 1)
                x1_low((n + 1) * KT - 1)
            low_mask(0)
            for m in range(KT):
                c_low(m)
            low_mask(1)

            def down_weights(u, parity, t):
                if not (isinstance(u, int) and u < 2):
                    dve.wait_ge(s["down_done"], u - 1)
                dve.tensor_copy(d_w[:, parity, :].unsqueeze(1), wd_raw[:, bass.ds(t, 1), :]).then_inc(s["d_w_made"], 1)

            for m in range(KT, 2 * KT):
                c_low(m)
            dve.wait_ge(down_in, 16)
            dve.wait_ge(s["c_done"], 2 * KT)

            def hidden(u, t, parity):
                dve.wait_ge(s["gact_made"], u + 1)
                dve.wait_ge(s["up_done"], u + 1)
                if not (isinstance(u, int) and u < 2):
                    dve.wait_ge(s["h_lo_made"], u - 1)
                dve.tensor_tensor(h[:, parity, :], gact[:, parity, :], bank[2 * parity + 1][:, :], ALU.mult
                                  ).then_inc(s["h_made"], 1)
                down_weights(u, parity, t)
                dve.wait_ge(s["h_hi_made"], u + 1)
                dve.tensor_tensor(h_lo[:, parity, :], h[:, parity, :], h_hi[:, parity, :].bitcast(F32), ALU.subtract
                                  ).then_inc(s["h_lo_made"], 1)

            def hidden_last(u, t, parity):
                dve.wait_ge(s["h_lo_made"], u - 1)
                down_weights(u, parity, t)
                for i, tok in enumerate(HALVES):
                    dve.wait_ge(s["gact_made"], u + 1 + i)
                    dve.wait_ge(s["up_done"], u + 1 + i)
                    dve.tensor_tensor(h[:, parity, tok], gact[:, parity, tok], bank[3 - 2 * i][:, tok], ALU.mult
                                      ).then_inc(s["h_made"], 1)
                    dve.wait_ge(s["h_hi_made"], u + 1 + i)
                    dve.tensor_tensor(h_lo[:, parity, tok], h[:, parity, tok], h_hi[:, parity, tok].bitcast(F32),
                                      ALU.subtract).then_inc(s["h_lo_made"], 1)

            def out_sum_last():
                for i, tok in enumerate(HALVES):
                    for m in range(KT):
                        at = x[:, m, N + tok.start:N + tok.stop]
                        dve.wait_ge(s["last_done"], KT * i + m + 1)
                        dve.tensor_tensor(at, bank[KT + m][:, tok], at, ALU.add).then_inc(s["out_made"], 1)

            def out_sum(n):
                for m in range(KT):
                    at = x[:, m, n * N:(n + 1) * N]
                    if m < KT - 1:
                        dve.wait_ge(s["sum_done"], (KT - 1) * n + m + 1)
                    else:
                        dve.wait_ge(s["down_done"], (n + 1) * MT)
                    dve.tensor_tensor(at, bank[KT + m][:, :], at, ALU.add).then_inc(s["out_made"], 1)

            for n in range(NH):
                base = n * MT
                hidden(base, 0, 0)
                if n:
                    out_sum(n - 1)
                hidden(base + 1, 1, 1)
                with dve.Fori(1, MT // 2 - n) as i:
                    hidden(base + 2 * i, 2 * i, 0)
                    hidden(base + 2 * i + 1, 2 * i + 1, 1)
                if n:
                    hidden(base + MT - 2, MT - 2, 0)
                    hidden_last(base + MT - 1, MT - 1, 1)
            out_sum_last()

        @block.tensor
        def _(pe):
            def keep_warm(count):
                for _ in range(count):
                    pe.matmul(bank[0][:, :], idle[:, 0:P], idle[:, :], start=True, stop=True)

            pe.wait_ge(s["idle_set"], 1)
            keep_warm(WARM_START)
            pe.wait_ge(lora_in, 16)
            for t in DELTA_ORDER:
                if t == DELTA_ORDER[2]:
                    pe.wait_ge(s["ones_set"], 1)
                    pe.wait_ge(s["place_made"], 1)
                    pe.matmul(bank[3][:, 0:2 * CODES], ones[:, :], place[:, :], start=True, stop=True
                              ).then_inc(s["jump_made"], 1)
                pe.matmul(delta[t][:, :], lora[:, D + t * P:D + (t + 1) * P], lora[:, 0:D], start=True, stop=True
                          ).then_inc(s["delta_made"], 1)

            def turn(g, k):
                return pe.transpose(wc[k][:, g * P:(g + 1) * P], ad_raw[:, g, k * P:(k + 1) * P],
                                    con[:, C_ID:C_ID + P])

            def add_jump(e, parity):
                pe.wait_ge(s["diag_made"], 2 * e + 2)
                for t in range(KT):
                    if t % 2 == 0:
                        pe.wait_ge(s["above_made"], 2 * e - 3 + t // 2)
                    for part in range(2):
                        mm = pe.matmul(acc[t][:, :], diag[:, parity, part, :], above[:, parity, t, :],
                                       start=False, stop=False, skip_group_check=True)
                    mm.then_inc(s["acc_used"], 1)

            pe.wait_ge(s["jump_read"], 1)
            for i, (e, t) in enumerate(FIRST):
                if i == 2:
                    pe.wait_ge(con_in, 16)
                    pe.wait_ge(s["dsb_made"], KT)
                    for g in range(NG - 1):
                        pe.wait_ge(ad_in[g], 16)
                        for k in range(KT):
                            turn(g, k)
                pe.wait_ge(s["diag_made"], 2 * e + 2)
                pe.wait_ge(s["above_first"], i + 1)
                for part in range(2):
                    mm = pe.matmul(acc[t][:, :], diag[:, e, part, :], above[:, e, t, :],
                                   start=(e == 0 and part == 0), stop=False, skip_group_check=True)
                mm.then_inc(s["acc_used"], 1)
            pe.wait_ge(ad_in[NG - 1], 16)
            for k in range(KT):
                turn(NG - 1, k).then_inc(s["adt_psum"], 1)
            pe.wait_ge(s["pairs_made"], 2)
            pairs = pe.value_load(npairs[0:1, 0:1], min_val=1, max_val=CODES // 2 - 1)
            with pe.Fori(0, pairs) as j:
                add_jump(2 * j + 2, 0)
                add_jump(2 * j + 3, 1)
            def three(dst, w_hi, w_lo, v_hi, v_lo, start, stop):
                pe.matmul(dst, w_hi, v_hi, start=start, stop=False)
                pe.matmul(dst, w_hi, v_lo, start=False, stop=False)
                return pe.matmul(dst, w_lo, v_hi, start=False, stop=stop)

            for t in range(KT):
                if t == 0:
                    pe.wait_ge(s["quant_first"], 1)
                    pe.wait_ge(s["w2t_made"], 1)
                else:
                    pe.wait_ge(s["w2t_lo_made"], t)
                    pe.wait_ge(s["w01_lo_made"], t)
                for k in range(KT):
                    at = slice(k * P, (k + 1) * P)
                    if t == 0:
                        pe.wait_ge(s["adt_made"], k + 1)
                        if k == KT // 2:
                            pe.wait_ge(s["quant"], 1)
                        pe.matmul(wc[k][:, :], w01[:, 0, at], w2t[:, 0, :], start=True, stop=False)
                    else:
                        mm = three(wc[k][:, :], w01_hi[:, t - 1, at], w01_lo[:, t - 1, at],
                                   w2t_hi[:, t - 1, :], w2t_lo[:, t - 1, :], False, t == KT - 1)
                    if t == KT - 1:
                        mm.then_inc(s["wc_done"], 1)

            for k in range(KT):
                pe.wait_ge(s["wc_hi_made"], k + 1)
                pe.wait_ge(s["wc_lo_made"], k + 1)
                pe.wait_ge(s["x_lo_made"], k + 1)
                for m in range(KT):
                    mm = three(bank[m][:, :], wc_hi[:, k, m * P:(m + 1) * P], wc_lo[:, k, m * P:(m + 1) * P],
                               x_hi[:, k, 0:N], x_lo[:, k, 0:N], k == 0, k == KT - 1)
                    if k == KT - 1:
                        mm.then_inc(s["x1_done"], 1)
            for m in range(KT):
                for k in range(KT):
                    mm = three(bank[KT + m][:, :], wc_hi[:, k, m * P:(m + 1) * P], wc_lo[:, k, m * P:(m + 1) * P],
                               x_hi[:, k, N:T], x_lo[:, k, N:T], k == 0, k == KT - 1)
                mm.then_inc(s["x1_done"], 1)

            for n in range(NH):
                pe.wait_ge(s["x1_lo_made"], (n + 1) * KT)
                for gg in range(2):
                    g = 2 * n + gg
                    for k in range(KT):
                        mm = three(bank[KT * n + 3][:, gg * TG:(gg + 1) * TG], ad_hi[:, k, g * P:(g + 1) * P],
                                   ad_lo[:, k, g * P:(g + 1) * P], x1_hi[:, k, g * TG:(g + 1) * TG],
                                   x1_lo[:, k, g * TG:(g + 1) * TG], k == 0, k == KT - 1)
                mm.then_inc(s["low_done"], 1)
                for m in range(KT):
                    if m == KT - 1:
                        pe.wait_ge(s["ad_m_made"], n + 1)
                    for k in range(KT):
                        three(bank[KT * n + m][:, :], w1_hi[:, k, m * P:(m + 1) * P], w1_lo[:, k, m * P:(m + 1) * P],
                              x1_hi[:, k, n * N:(n + 1) * N], x1_lo[:, k, n * N:(n + 1) * N], k == 0, False)
                    pe.wait_ge(s["ad_mlo_made"], n + 1)
                    for gg in range(2):
                        g = 2 * n + gg
                        mm = three(bank[KT * n + m][:, gg * TG:(gg + 1) * TG], bd_hi[:, g, m * P:(m + 1) * P],
                                   bd_lo[:, g, m * P:(m + 1) * P], ad_mhi[:, gg * TG:(gg + 1) * TG],
                                   ad_mlo[:, gg * TG:(gg + 1) * TG], False, gg == 1)
                    mm.then_inc(s["c_done"], 1)

            def gate_up(u, parity, n):
                tok = slice(n * N, (n + 1) * N)
                for part in range(2):
                    pe.wait_ge(s["gu_w_made"], 2 * u + part + 1)
                    if not (isinstance(u, int) and u < 2):
                        if part == 0:
                            pe.wait_ge(s["h_made"], u - 1)
                    for k in range(KT):
                        w = gu_w[:, parity, part, k, :]
                        pe.matmul(bank[2 * parity + part][:, :], w, c_hi[:, k, tok], start=(k == 0), stop=False)
                        mm = pe.matmul(bank[2 * parity + part][:, :], w, c_lo[:, k, tok], start=False,
                                       stop=(k == KT - 1))
                    mm.then_inc(s["up_done" if part else "gate_done"], 1)

            def gate_up_last(u, parity, n):
                for i, tok in enumerate(HALVES):
                    at = slice(n * N + tok.start, n * N + tok.stop)
                    for part in range(2):
                        pe.wait_ge(s["gu_w_made"], 2 * u + part + 1)
                        pe.wait_ge(s["h_made"], u - 1 + i)
                        for k in range(KT):
                            w = gu_w[:, parity, part, k, :]
                            pe.matmul(bank[2 - 2 * i + part][:, tok], w, c_hi[:, k, at], start=(k == 0), stop=False)
                            mm = pe.matmul(bank[2 - 2 * i + part][:, tok], w, c_lo[:, k, at], start=False,
                                           stop=(k == KT - 1))
                        mm.then_inc(s["up_done" if part else "gate_done"], 1)

            def down_last(u):
                pe.wait_ge(s["d_w_made"], u + 1)
                for i, tok in enumerate(HALVES):
                    pe.wait_ge(s["h_hi_made"], u + 1 + i)
                    pe.wait_ge(s["h_lo_made"], u + 1 + i)
                    for m in range(KT):
                        if i:
                            pe.wait_ge(s["out_made"], KT + m + 1)
                        for parity in range(2):
                            w = d_w[:, parity, m * P:(m + 1) * P]
                            pe.matmul(bank[KT + m][:, tok], w, h_hi[:, parity, tok], start=False, stop=False,
                                      skip_group_check=True)
                            mm = pe.matmul(bank[KT + m][:, tok], w, h_lo[:, parity, tok], start=False,
                                           stop=(parity == 1), skip_group_check=True)
                        mm.then_inc(s["last_done"], 1)

            def down(u, parity, first=False, last=False):
                pe.wait_ge(s["d_w_made"], u + 1)
                pe.wait_ge(s["h_hi_made"], u + 1)
                pe.wait_ge(s["h_lo_made"], u + 1)
                for m in range(KT):
                    w = d_w[:, parity, m * P:(m + 1) * P]
                    pe.matmul(bank[KT + m][:, :], w, h_hi[:, parity, :], start=first, stop=False,
                              skip_group_check=True)
                    mm = pe.matmul(bank[KT + m][:, :], w, h_lo[:, parity, :], start=False, stop=last,
                                   skip_group_check=True)
                    if last and m < KT - 1:
                        mm.then_inc(s["sum_done"], 1)
                mm.then_inc(s["down_done"], 1)

            for n in range(NH):
                base = n * MT
                if n == 0:
                    pe.wait_ge(s["c_lo_made"], KT)
                    gate_up(0, 0, 0)
                gate_up(base + 1, 1, n)
                if n:
                    pe.wait_ge(s["out_made"], KT)
                else:
                    pe.wait_ge(s["c_lo_made"], 2 * KT)
                down(base, 0, first=True)
                with pe.Fori(1, MT // 2 - n) as i:
                    gate_up(base + 2 * i, 0, n)
                    down(base + 2 * i - 1, 1)
                    gate_up(base + 2 * i + 1, 1, n)
                    down(base + 2 * i, 0)
                if n == 0:
                    gate_up(base + MT, 0, n + 1)
                    down(base + MT - 1, 1, last=True)
                else:
                    gate_up(base + MT - 2, 0, n)
                    down(base + MT - 3, 1)
                    gate_up_last(base + MT - 1, 1, n)
                    down_last(base + MT - 1)


def host_constants(np):
    con = np.zeros((P, C_N), np.float32)
    con[:, C_ID:C_ID + P] = np.eye(P)
    rows, toks = np.arange(P)[:, None], np.arange(TG)[None, :]
    con[:, C_BM:C_BM + TG] = np.where(rows // R1 == toks // TB, LORA1, 0.0)
    con[:CODES, C_TRI:C_TRI + CODES] = np.tril(np.ones((CODES, CODES)))
    con[:, C_IOTA:C_IOTA + CODES] = np.arange(1, CODES + 1)
    return con


def kernel(**inputs):
    import numpy as np
    import concourse.bacc as bacc
    from concourse import mybir as mb
    from concourse.bass_utils import run_bass_kernel_spmd as run

    v = {k: np.asarray(x) for k, x in inputs.items()}
    arrays = {
        "codebook": v["condB_codebook"].reshape(1, CODES),
        "slog": v["L0_cond_scale_log"].reshape(2, P, 2, CG).transpose(1, 0, 2, 3).reshape(P, KT * CG),
        "lora": np.concatenate([v["L0_cond_lora_A"], v["L0_cond_lora_B"].reshape(2, P, 2, RANK0).transpose(
            3, 0, 2, 1).reshape(RANK0, D)], axis=1),
        "con": host_constants(np),
        "w0": v["L0_cond_weight"].reshape(2, P, 2, D).transpose(0, 2, 1, 3).reshape(KT, P, D),
        "slot": np.concatenate([np.repeat(v["itok_B_0_23"], R1).reshape(NG, P).T,
                                (np.arange(P, dtype=np.int32) % R1)[:, None]], axis=1),
        "q4": v["L0_ffn_weight_q4"].reshape(D, D // 2).T,
        "s2": v["L0_ffn_weight_scale"].reshape(D, D // GRP).T,
        "x": v["x"].reshape(T, D).T,
        "w1": v["L1_cond_W"].T,
        "bias0": v["L0_ffn_bias"].reshape(KT, P).T,
        "bias1": v["L1_cond_b"].reshape(KT, P).T,
        "lora1_a": v["L1_cond_lora_As"].transpose(0, 2, 1).reshape(SLOTS * R1, D),
        "lora1_b": v["L1_cond_lora_Bs"].reshape(SLOTS * R1, D),
        "wg": v["L1_ffn_W_gate"].T,
        "wu": v["L1_ffn_W_up"].T,
        "wd": v["L1_ffn_W_down"].T,
    }
    arrays = {k: np.ascontiguousarray(x) for k, x in arrays.items()}
    nc = bacc.Bacc("TRN2", target_bir_lowering=False, num_devices=1)
    aps = {k: nc.dram_tensor("in_" + k, x.shape, mb.dt.from_np(x.dtype), kind="ExternalInput").ap()
           for k, x in arrays.items()}
    out = nc.dram_tensor("out_t", (D, T), mb.dt.float32, kind="ExternalOutput").ap()
    build_program(nc, aps, out)
    got = run(nc, [{"in_" + k: x for k, x in arrays.items()}], core_ids=[0]).results[0]["out_t"]
    return np.ascontiguousarray(np.asarray(got).T).reshape(B, TB, D)
```
